# Optimizing a Trainium2 kernel written in Bass

```python
import numpy as np
import jax
import jax.numpy as jnp

def _softmax(x, axis=-1):
    return jax.nn.softmax(x, axis=axis)

def _gelu(x):
    return jax.nn.gelu(x, approximate=True)

def _silu(x):
    return jax.nn.silu(x)

def _sigmoid(x):
    return jax.nn.sigmoid(x)

def _layernorm(x, axis=-1, eps=1e-05):
    m = jnp.mean(x, axis=axis, keepdims=True)
    v = jnp.var(x, axis=axis, keepdims=True)
    return (x - m) / jnp.sqrt(v + eps)

def _scatter_add(tgt, idx, src, axis=0):
    return tgt.at[idx].add(src)

def _segment_sum(src, seg, n):
    return jax.ops.segment_sum(src, seg, n)
kernel_name = 'mk_flamingo_gated_d1_seqx_r4_8274e6'

def setup_inputs(seed: int=0):
    np.random.seed(seed)
    _w = jnp.asarray

    def _rec_inputs():
        import jax
        import jax.numpy as jnp
        _rk = jax.random.key(seed)
        x = 7.22e-05 + 1 * jax.random.normal(jax.random.fold_in(_rk, 1), (32, 256, 256), jnp.float32)
        _lenS = 256 - jax.random.randint(jax.random.fold_in(_rk, 7), (32,), 0, max(1, 256 // 4) + 1, jnp.int32)
        _lenS2 = 256 - jax.random.randint(jax.random.fold_in(_rk, 8), (32,), 0, max(1, 256 // 4) + 1, jnp.int32)
        _ctx_1024P = jax.random.normal(jax.random.fold_in(_rk, 11), (32, 16, 256), jnp.float32)
        _ctx_1024c = jax.random.dirichlet(jax.random.fold_in(_rk, 511), 0.3 * jnp.ones((16,), jnp.float32), (32, 256))
        _ctx_1024t = jnp.einsum('bsk,bkd->bsd', _ctx_1024c, _ctx_1024P)
        _ctx_1024t = _ctx_1024t * jax.lax.rsqrt(jnp.mean(jnp.square(_ctx_1024t)) + 1e-12) * 0.953939
        ctx_1024 = 4.13588e-05 + 0.999923 * (_ctx_1024t + 0.3 * jax.random.normal(jax.random.fold_in(_rk, 611), (32, 256, 256), jnp.float32))
        _g = jax.random.normal(jax.random.fold_in(_rk, 9001), (2, 1), jnp.float32)
        _g = jnp.sign(_g) * jnp.maximum(jnp.abs(_g), 1.0) + (_g == 0) * 1.0
        g_xattn = _g[0]
        g_ffn = _g[1]
        return (x, ctx_1024, g_xattn, g_ffn)
    x, ctx_1024, g_xattn, g_ffn = _rec_inputs()

    def _L0_xattn_setup():
        import jax, jax.numpy as jnp
        import numpy as np
        D_MODEL = 256
        NUM_HEADS = 16
        KERNEL_EPS = 0.0001
        NORM_STAB = 1e-06

        def _performer_forward(query, key, value, random_features):
            B, L, dm = query.shape
            h = NUM_HEADS
            d = dm // h
            m = random_features.shape[1]

            def split_heads(x):
                return x.reshape(B, L, h, d).transpose(0, 2, 1, 3)
            q, k, v = (split_heads(query), split_heads(key), split_heads(value))
            scale = dm ** (-0.25)
            q = q * scale
            k = k * scale
            proj_q = jnp.einsum('bhld,dm->bhlm', q, random_features)
            proj_k = jnp.einsum('bhld,dm->bhlm', k, random_features)
            h_q = -0.5 * jnp.sum(q * q, axis=-1, keepdims=True)
            h_k = -0.5 * jnp.sum(k * k, axis=-1, keepdims=True)
            q_stab = h_q
            k_stab = jnp.max(h_k)
            q_kernel = jnp.exp(h_q + (proj_q - q_stab))
            k_kernel = jnp.exp(h_k + (proj_k - k_stab))
            nc = m ** (-0.5)
            q_prime = nc * (q_kernel + KERNEL_EPS)
            k_prime = nc * (k_kernel + KERNEL_EPS)
            qp = q_prime.transpose(2, 0, 1, 3)
            kp = k_prime.transpose(2, 0, 1, 3)
            vp = v.transpose(2, 0, 1, 3)

            def step(carry, inp):
                S, Z = carry
                qt, kt, vt = inp
                S = S + kt[..., :, None] * vt[..., None, :]
                Z = Z + kt
                num = jnp.einsum('bhm,bhmd->bhd', qt, S)
                den = jnp.einsum('bhm,bhm->bh', qt, Z)
                return ((S, Z), (num, den))
            S0 = jnp.zeros((B, h, m, d), q_prime.dtype)
            Z0 = jnp.zeros((B, h, m), q_prime.dtype)
            _, (nums, dens) = jax.lax.scan(step, (S0, Z0), (qp, kp, vp))
            nums = nums.transpose(1, 2, 0, 3)
            dens = dens.transpose(1, 2, 0)[..., None]
            extreme = (jnp.abs(dens) <= NORM_STAB).astype(dens.dtype)
            dens = dens + 2.0 * NORM_STAB * extreme
            out = nums / dens
            return out.transpose(0, 2, 1, 3).reshape(B, L, dm)
        key = jax.random.key(seed)
        k1, k2, k3, k4 = jax.random.split(key, 4)
        B, L = (4, 512)
        d_head, m = (D_MODEL // NUM_HEADS, 64)
        return {'query': jax.random.normal(k1, (B, L, D_MODEL), jnp.float32), 'key': jax.random.normal(k2, (B, L, D_MODEL), jnp.float32), 'value': jax.random.normal(k3, (B, L, D_MODEL), jnp.float32), 'random_features': jax.random.normal(k4, (d_head, m), jnp.float32)}
    _L0_xattn_all = _L0_xattn_setup()
    _L0_xattn_in = {k: v for k, v in _L0_xattn_all.items() if k in ('random_features',)}
    del _L0_xattn_all

    def _L0_ffn_setup():
        import jax, jax.numpy as jnp
        import numpy as np
        D = 256
        H = 16
        HD = D // H
        L = 64
        E = 8
        B, T = (4, 512)
        EPS = 1e-06

        def _glorot(k, shape):
            fan_in, fan_out = (shape[-2], shape[-1])
            lim = np.sqrt(6.0 / (fan_in + fan_out)).astype(np.float32)
            return jax.random.uniform(k, shape, jnp.float32, -lim, lim)

        def _rmsnorm(x, gamma):
            return gamma * x * jax.lax.rsqrt(jnp.mean(x * x, axis=-1, keepdims=True) + EPS)
        key = jax.random.key(seed)
        ks = jax.random.split(key, 8)
        return {'x': jax.random.normal(ks[0], (B, T, D), jnp.float32), 'gamma1': jnp.ones((D,), jnp.float32), 'Wq': _glorot(ks[1], (D, D)), 'bq': jnp.zeros((D,), jnp.float32), 'Wdown': _glorot(ks[2], (D, L)), 'bdown': jnp.zeros((L,), jnp.float32), 'Wup': _glorot(ks[3], (L, 2 * D)), 'bup': jnp.zeros((2 * D,), jnp.float32), 'Wo': _glorot(ks[4], (D, D)), 'bo': jnp.zeros((D,), jnp.float32), 'gamma2': jnp.ones((D,), jnp.float32), 'Wg': _glorot(ks[5], (D, E)), 'bg': jnp.zeros((E,), jnp.float32), 'We': _glorot(ks[6], (E, D, D))}
    _L0_ffn_all = _L0_ffn_setup()
    _L0_ffn_in = {k: v for k, v in _L0_ffn_all.items() if k in ('gamma1', 'Wq', 'bq', 'Wdown', 'bdown', 'Wup', 'bup', 'Wo', 'bo', 'gamma2', 'Wg', 'bg', 'We')}
    del _L0_ffn_all
    return {'x': x, 'ctx_1024': ctx_1024, 'g_xattn': g_xattn, 'g_ffn': g_ffn, 'L0_xattn_random_features': _L0_xattn_in['random_features'], 'L0_ffn_gamma1': _L0_ffn_in['gamma1'], 'L0_ffn_Wq': _L0_ffn_in['Wq'], 'L0_ffn_bq': _L0_ffn_in['bq'], 'L0_ffn_Wdown': _L0_ffn_in['Wdown'], 'L0_ffn_bdown': _L0_ffn_in['bdown'], 'L0_ffn_Wup': _L0_ffn_in['Wup'], 'L0_ffn_bup': _L0_ffn_in['bup'], 'L0_ffn_Wo': _L0_ffn_in['Wo'], 'L0_ffn_bo': _L0_ffn_in['bo'], 'L0_ffn_gamma2': _L0_ffn_in['gamma2'], 'L0_ffn_Wg': _L0_ffn_in['Wg'], 'L0_ffn_bg': _L0_ffn_in['bg'], 'L0_ffn_We': _L0_ffn_in['We']}

def reference(x, ctx_1024, g_xattn, g_ffn, L0_xattn_random_features, L0_ffn_gamma1, L0_ffn_Wq, L0_ffn_bq, L0_ffn_Wdown, L0_ffn_bdown, L0_ffn_Wup, L0_ffn_bup, L0_ffn_Wo, L0_ffn_bo, L0_ffn_gamma2, L0_ffn_Wg, L0_ffn_bg, L0_ffn_We):
    import jax
    import jax.numpy as jnp

    def _L0_xattn_ref(query, key, value, random_features):
        import jax, jax.numpy as jnp
        import numpy as np
        D_MODEL = 256
        NUM_HEADS = 16
        KERNEL_EPS = 0.0001
        NORM_STAB = 1e-06

        def _performer_forward(query, key, value, random_features):
            B, L, dm = query.shape
            h = NUM_HEADS
            d = dm // h
            m = random_features.shape[1]

            def split_heads(x):
                return x.reshape(B, L, h, d).transpose(0, 2, 1, 3)
            q, k, v = (split_heads(query), split_heads(key), split_heads(value))
            scale = dm ** (-0.25)
            q = q * scale
            k = k * scale
            proj_q = jnp.einsum('bhld,dm->bhlm', q, random_features)
            proj_k = jnp.einsum('bhld,dm->bhlm', k, random_features)
            h_q = -0.5 * jnp.sum(q * q, axis=-1, keepdims=True)
            h_k = -0.5 * jnp.sum(k * k, axis=-1, keepdims=True)
            q_stab = h_q
            k_stab = jnp.max(h_k)
            q_kernel = jnp.exp(h_q + (proj_q - q_stab))
            k_kernel = jnp.exp(h_k + (proj_k - k_stab))
            nc = m ** (-0.5)
            q_prime = nc * (q_kernel + KERNEL_EPS)
            k_prime = nc * (k_kernel + KERNEL_EPS)
            qp = q_prime.transpose(2, 0, 1, 3)
            kp = k_prime.transpose(2, 0, 1, 3)
            vp = v.transpose(2, 0, 1, 3)

            def step(carry, inp):
                S, Z = carry
                qt, kt, vt = inp
                S = S + kt[..., :, None] * vt[..., None, :]
                Z = Z + kt
                num = jnp.einsum('bhm,bhmd->bhd', qt, S)
                den = jnp.einsum('bhm,bhm->bh', qt, Z)
                return ((S, Z), (num, den))
            S0 = jnp.zeros((B, h, m, d), q_prime.dtype)
            Z0 = jnp.zeros((B, h, m), q_prime.dtype)
            _, (nums, dens) = jax.lax.scan(step, (S0, Z0), (qp, kp, vp))
            nums = nums.transpose(1, 2, 0, 3)
            dens = dens.transpose(1, 2, 0)[..., None]
            extreme = (jnp.abs(dens) <= NORM_STAB).astype(dens.dtype)
            dens = dens + 2.0 * NORM_STAB * extreme
            out = nums / dens
            return out.transpose(0, 2, 1, 3).reshape(B, L, dm)
        return _performer_forward(query, key, value, random_features)

    def _L0_ffn_ref(x, gamma1, Wq, bq, Wdown, bdown, Wup, bup, Wo, bo, gamma2, Wg, bg, We):
        import jax, jax.numpy as jnp
        import numpy as np
        D = 256
        H = 16
        HD = D // H
        L = 64
        E = 8
        B, T = (4, 512)
        EPS = 1e-06

        def _glorot(k, shape):
            fan_in, fan_out = (shape[-2], shape[-1])
            lim = np.sqrt(6.0 / (fan_in + fan_out)).astype(np.float32)
            return jax.random.uniform(k, shape, jnp.float32, -lim, lim)

        def _rmsnorm(x, gamma):
            return gamma * x * jax.lax.rsqrt(jnp.mean(x * x, axis=-1, keepdims=True) + EPS)
        b, t = (x.shape[0], x.shape[1])
        h = _rmsnorm(x, gamma1)
        q = (h @ Wq + bq).reshape(b, t, H, HD)
        kv = ((h @ Wdown + bdown) @ Wup + bup).reshape(b, t, H, 2 * HD)
        k, v = jnp.split(kv, 2, axis=-1)
        att = jnp.einsum('bthd,btgd->bthg', q, k) / np.sqrt(HD).astype(np.float32)
        att = jax.nn.softmax(att, axis=-1)
        out = jnp.einsum('bthg,btgd->bthd', att, v).reshape(b, t, D)
        x = x + (out @ Wo + bo)
        h2 = _rmsnorm(x, gamma2)
        gate = jax.nn.softmax(h2 @ Wg + bg, axis=-1)
        combined = jnp.einsum('btd,edf,bte->btf', h2, We, gate)
        return x + combined
    x = x + jnp.tanh(g_xattn[0]) * _L0_xattn_ref(_layernorm(x, axis=-1), ctx_1024, ctx_1024, L0_xattn_random_features)
    x = x + jnp.tanh(g_ffn[0]) * _L0_ffn_ref(_layernorm(x, axis=-1), L0_ffn_gamma1, L0_ffn_Wq, L0_ffn_bq, L0_ffn_Wdown, L0_ffn_bdown, L0_ffn_Wup, L0_ffn_bup, L0_ffn_Wo, L0_ffn_bo, L0_ffn_gamma2, L0_ffn_Wg, L0_ffn_bg, L0_ffn_We)
    return x

_drawn_inputs = setup_inputs


def setup_inputs(seed=0):
    import zlib

    import numpy as np

    out = dict(_drawn_inputs(seed))
    spreads = {'L0_ffn_gamma1': (1.0, 0.2),
     'L0_ffn_bq': (0.0, 0.341),
     'L0_ffn_bdown': (0.0, 0.322),
     'L0_ffn_bup': (0.0, 0.1),
     'L0_ffn_bo': (0.0, 0.1),
     'L0_ffn_gamma2': (1.0, 0.2),
     'L0_ffn_bg': (0.0, 0.1)}
    factors = {}
    for name, (base, spread) in spreads.items():
        noise = np.random.default_rng([zlib.crc32(name.encode()), seed]).standard_normal(out[name].shape)
        drawn = base * np.exp(spread * noise) if base else spread * noise
        out[name] = jnp.asarray(drawn.astype(out[name].dtype))
    for name, factor in factors.items():
        out[name] = (out[name] * factor).astype(out[name].dtype)
    return out
```

```python
from contextlib import ExitStack

import concourse.bass as bass
from concourse import mybir

F32 = mybir.dt.float32
F32R = mybir.dt.float32r
ALU = mybir.AluOpType
ACT = mybir.ActivationFunctionType
AX = mybir.AxisListType

P = 128
NB, L, D = 32, 256, 256
T = L // P
C = D // P
H, HD = 16, 16
M = 64
PAIRS = H * M // P
QUADS = H // 4
E = 8
R = 64
KERNEL_EPS, NORM_STAB = 1e-4, 1e-6
LN_EPS, RMS_EPS = 1e-5, 1e-6
QK_SCALE = D ** -0.25
CH = 4


SEPARATE_WAIT = {("dve", "aggr"), ("pe", "small"), ("pool", "scalar"), ("sp", "")}


class Step:

    def __init__(self, name, eng, ns, waits, run, dma=False, kind=""):
        self.name, self.eng, self.ns, self.waits, self.run, self.dma = name, eng, ns, waits, run, dma
        self.kind = kind


class Batch:

    def __init__(self, i, k):
        self.i, self.k, self.par = i, k, k % 2

    def times(self, c, add=0):
        return self.i * (2 * c) + (self.k * c + add)

    def before(self, n):
        return Batch(self.i, self.k - n)

    def is_before_first(self, n):
        return isinstance(self.i, int) and 2 * self.i + self.k - n < 0


class Stream:

    def __init__(self, key, steps, new_sem):
        self.key, self.steps = key, steps
        self.per_batch, self.place, self.sems = {}, {}, {}
        for s in steps:
            if s.dma:
                self.sems[s.name] = [new_sem(f"{key}_{s.name}_{p}") for p in range(2)]
                continue
            self.per_batch[s.eng] = self.per_batch.get(s.eng, 0) + 1
            self.place[s.name] = self.per_batch[s.eng]
            if s.eng not in self.sems:
                self.sems[s.eng] = new_sem(f"{key}_{s.eng}")
        self.by_name = {s.name: s for s in steps}

    def target(self, name, batch):
        s = self.by_name[name]
        if s.dma:
            return self.sems[name][batch.par], 16, (batch.k // 2 + 1) * 16
        c = self.per_batch[s.eng]
        return self.sems[s.eng], 2 * c, batch.k * c + self.place[name]

    def emit(self, step, eng, batch, streams):
        needed = {}
        for w in step.waits:
            name = w.rstrip("-")
            back = len(w) - len(name)
            key, name = name.split(".")
            at = batch if key in "PFA" else Batch(0, 0)
            if at.is_before_first(back):
                continue
            sem, per_i, value = streams[key].target(name, at.before(back))
            per_i = per_i if key in "PFA" else 0
            if sem.name not in needed or needed[sem.name][2] < value:
                needed[sem.name] = (sem, per_i, value)
        waited = False
        for sem, per_i, value in needed.values():
            if waited and step.eng == "sp":
                eng.nop(nofuse=True)
            eng.wait_ge(sem, batch.i * per_i + value if per_i else value)
            waited = waited or bool(per_i) and not isinstance(batch.i, int)
        if waited and (step.eng, step.kind) in SEPARATE_WAIT:
            eng.nop(nofuse=True)
        last = step.run(eng, batch)
        if step.dma:
            last.then_inc(self.sems[step.name][batch.par], 16)
        else:
            last.then_inc(self.sems[step.eng], 1)


def merged(lists):
    free, done, order = {}, {}, []
    heads = [0] * len(lists)
    while any(h < len(l) for h, (_, l) in zip(heads, lists)):
        best = None
        for n, (key, l) in enumerate(lists):
            if heads[n] < len(l):
                s = l[heads[n]]
                start = max([free.get(s.eng, 0)] + [done.get(w, 0) for w in s.waits if w[0] == key])
                if best is None or start < best[0]:
                    best = (start, n, key, s)
        start, n, key, s = best
        heads[n] += 1
        free[s.eng] = start + s.ns
        done[f"{key}.{s.name}"] = start + s.ns + 150
        order.append((key, s))
    return order


P_BANKS = {
    "h_t": (0, "P.a_diag03-"), "q_exp0": (1, "P.a_cross3-"), "q_exp1": (2, "P.a_diag13-"),
    "q_exp2": (0, "P.h_t"), "q_exp3": (1, "P.q_exp0"), "k_exp0": (2, "P.q_exp1"),
    "k_exp1": (0, "P.q_exp2"), "k_exp2": (1, "P.q_exp3"), "k_exp3": (2, "P.k_exp0"),
    "a_diag00": (0, "P.k_exp1"), "a_cross0": (1, "P.k_exp2"), "a_diag10": (2, "P.k_exp3"),
    "a_diag01": (0, "P.a_diag00"), "a_cross1": (1, "P.a_cross0"), "a_diag11": (2, "P.a_diag10"),
    "a_diag02": (0, "P.a_diag01"), "a_cross2": (1, "P.a_cross1"), "a_diag12": (2, "P.a_diag11"),
    "a_diag03": (0, "P.a_diag02"), "a_cross3": (1, "P.a_cross2"), "a_diag13": (2, "P.a_diag12"),
}
F_BANKS = {
    "ht_lo0": (0, "F.e1_1b-"), "ht_lo1": (1, "F.e1_2b-"), "qk0": (2, "F.e1_3b-"),
    "qk1": (0, "F.ht_lo0"), "vv": (1, "F.ht_lo1"), "s_sub": (2, "F.qk0"), "o_tok": (0, "F.qk1"),
    "ot_lo": (1, "F.vv"), "y2": (2, "F.s_sub"), "h2_lo0": (0, "F.o_tok"), "h2_lo1": (1, "F.ot_lo"),
    "gl": (2, "F.y2"), "ga": (0, "F.h2_lo0"), "e0_0b": (1, "F.h2_lo1"), "e0_1b": (2, "F.gl"),
    "e0_2b": (0, "F.ga"), "e0_3b": (1, "F.e0_0b"), "e1_0b": (2, "F.e0_1b"), "e1_1b": (0, "F.e0_2b"),
    "e1_2b": (1, "F.e0_3b"), "e1_3b": (2, "F.e1_0b"),
}


def build(nc, x_d, ctx_d, gx_d, gf_d, rf_d, g1_d, wq_d, bq_d, wdn_d, bdn_d, wup_d, bup_d,
          wo_d, bo_d, g2_d, wg_d, bg_d, we_d, out_d):
    ctx = ExitStack()
    with ctx:
        def sb(name, shape, dt=F32):
            return ctx.enter_context(nc.sbuf_tensor(name, shape, dt))

        def sem(name):
            return ctx.enter_context(nc.semaphore(name))

        ctx.enter_context(nc.allow_non_contiguous_dma(reason="a few small parameter vectors"))

        p_ps = ctx.enter_context(nc.psum_tensor("p_ps", [P, 3, 512], F32))
        n_ps = ctx.enter_context(nc.psum_tensor("n_ps", [P, 2, 512], F32))
        f_ps = ctx.enter_context(nc.psum_tensor("f_ps", [P, 3, 512], F32))

        ident = sb("ident", [P, P])
        causal = sb("causal", [P, P])
        sel_tok = sb("sel_tok", [P, 2])
        neg_half = sb("neg_half", [P, 4])
        wf_hi, wf_lo = sb("wf_hi", [P, 4, P], F32R), sb("wf_lo", [P, 4, P], F32R)
        h_sel = sb("h_sel", [R, PAIRS, P], F32R)
        wqkv_hi, wqkv_lo = sb("wqkv_hi", [P, C, 3 * D], F32R), sb("wqkv_lo", [P, C, 3 * D], F32R)
        wo_hi, wo_lo = sb("wo_hi", [P, C, D], F32R), sb("wo_lo", [P, C, D], F32R)
        wg_hi, wg_lo = sb("wg_hi", [P, C, P], F32R), sb("wg_lo", [P, C, P], F32R)
        we_hi, we_lo = sb("we_hi", [P, C, E * D], F32R), sb("we_lo", [P, C, E * D], F32R)
        b_qkv = sb("b_qkv", [P, 3 * D])
        b_o = sb("b_o", [P, D])
        b_g = sb("b_g", [P, E])
        tanh_x, tanh_f = sb("tanh_x", [P, 1]), sb("tanh_f", [P, 1])
        g_cols = sb("g_cols", [P, 2])
        hk = sb("hk", [P, NB * T, H])
        hk_min, hk_col, stab = sb("hk_min", [P, 1]), sb("hk_col", [P, 1]), sb("stab", [P, 1])

        streams = {}

        early = ExitStack()
        stage = early.enter_context(nc.sbuf_tensor("stage", [P, C * E * D], F32))
        c_chunk = [early.enter_context(nc.sbuf_tensor(f"c_chunk{p}", [P, CH * T, D], F32)) for p in range(2)]
        stage_q = early.enter_context(nc.sbuf_tensor("stage_q", [P, C, D], F32))
        stage_o = early.enter_context(nc.sbuf_tensor("stage_o", [P, C, D], F32))
        qkv32 = early.enter_context(nc.sbuf_tensor("qkv32", [P, C, 3 * D], F32))
        stage_o2 = early.enter_context(nc.sbuf_tensor("stage_o2", [P, 2 * D], F32))
        early.close()
        bn6f, mvf = sb("bn6f", [P, T, 6]), sb("mvf", [P, T, 2])
        var_f, r_f = sb("var_f", [P, 2, T]), sb("r_f", [P, 2, T])
        y, yb, hn = sb("y", [P, T, D]), sb("yb", [P, T, D]), sb("hn", [P, T, D])
        ht_hi, ht_lo = sb("ht_hi", [P, C, L], F32R), sb("ht_lo", [P, C, L], F32R)
        qkv = sb("qkv", [P, T, 3 * D])
        q_t, k_t, v_t = sb("q_t", [P, H, 32]), sb("k_t", [P, H, 32]), sb("v_t", [P, HD, 32])
        q_bd = sb("q_bd", [P, T, H, 32])
        s_max, s_sub = sb("s_max", [P, 32]), sb("s_sub", [P, 32, H])
        s_exp, s_sum, s_rec = sb("s_exp", [P, 32, H]), sb("s_sum", [P, 32]), sb("s_rec", [P, 32])
        p_bd, p_t = sb("p_bd", [P, 32, T, H]), sb("p_t", [P, 32, 32])
        o_tok = sb("o_tok", [P, T, D])
        ot_hi, ot_lo = sb("ot_hi", [P, C, L], F32R), sb("ot_lo", [P, C, L], F32R)
        y2 = sb("y2", [P, T, D])
        ms, r2 = sb("ms", [P, T]), sb("r2", [P, T])
        h2n = sb("h2n", [P, T, D])
        h2_hi, h2_lo = sb("h2_hi", [P, C, L], F32R), sb("h2_lo", [P, C, L], F32R)
        gl = sb("gl", [E, L])
        ga, gb, gate = sb("ga", [P, T, E]), sb("gb", [P, T, E]), sb("gate", [P, T, E])
        gm, gr = sb("gm", [P, T]), sb("gr", [P, T])
        acc = [[sb(f"acc{t}_{n}", [P, D]) for n in range(2)] for t in range(T)]
        outb = [sb(f"outb{n}", [P, T, D]) for n in range(2)]

        stage_d = sb("stage_d", [P, C, R])
        stage_u = sb("stage_u", [R, 2 * D])
        stage_g = sb("stage_g", [P, C, P])
        stage_f = sb("stage_f", [P, 4, P])
        wdn_t = sb("wdn_t", [R, C, P])
        bdn_col, bdn_wide = sb("bdn_col", [R, 1]), sb("bdn_wide", [R, P])
        gamma1, gamma2 = sb("gamma1", [P, C]), sb("gamma2", [P, C])

        W = []

        def w(name, eng, waits, run, dma=False):
            W.append(Step(name, eng, 100, waits, run, dma))

        def const_tri(e, b):
            return e.affine_select(out=causal[:, :], in_=causal[:, :], compare_op=ALU.is_ge, fill=0.0,
                                   base=0, pattern=[[1, P]], channel_multiplier=-1)

        w("zero_id", "pool", [], lambda e, b: e.memset(ident[:, :], 0.0))
        w("one_tri", "pool", [], lambda e, b: e.memset(causal[:, :], 1.0))
        w("zero_f", "dve", [], lambda e, b: e.memset(stage_f[:, :, :], 0.0))
        w("zero_g", "dve", [], lambda e, b: e.memset(stage_g[:, :, :], 0.0))
        w("half", "dve", [], lambda e, b: e.memset(neg_half[:, :], -0.5))
        w("ident", "pool", ["W.zero_id"], lambda e, b: e.affine_select(
            out=ident[:, :], in_=ident[:, :], compare_op=ALU.not_equal, fill=1.0, base=0,
            pattern=[[-1, P]], channel_multiplier=1))
        w("tri", "pool", ["W.one_tri"], const_tri)

        w("h_sel", "dve", ["W.ident"], lambda e, b: e.tensor_tensor(
            h_sel[:, :, :].rearrange("p a (e m) -> p (a e) m", m=M),
            ident[0:R, 0:H].unsqueeze(2).to_broadcast([R, H, M]),
            ident[0:R, 32:32 + H].unsqueeze(2).to_broadcast([R, H, M]), ALU.add))

        loads = [
            ("ld_gx", lambda: (g_cols[:, 0:1], gx_d.rearrange("(a n) -> a n", a=1).to_broadcast([P, 1]))),
            ("ld_gf", lambda: (g_cols[:, 1:2], gf_d.rearrange("(a n) -> a n", a=1).to_broadcast([P, 1]))),
            ("ld_g1", lambda: (gamma1[:, :], g1_d.rearrange("(c p) -> p c", p=P))),
            ("ld_g2", lambda: (gamma2[:, :], g2_d.rearrange("(c p) -> p c", p=P))),
            ("ld_q", lambda: (stage_q[:, :, :], wq_d.rearrange("(c p) n -> p c n", p=P))),
            ("ld_dn", lambda: (stage_d[:, :, :], wdn_d.rearrange("(c p) n -> p c n", p=P))),
            ("ld_bdn", lambda: (bdn_col[:, :], bdn_d.rearrange("(p a) -> p a", a=1))),
            ("ld_up", lambda: (stage_u[:, :], wup_d)),
            ("ld_bq", lambda: (b_qkv[:, 0:D], bq_d.rearrange("(a n) -> a n", a=1).to_broadcast([P, D]))),
            ("ld_bup", lambda: (b_qkv[:, D:3 * D], bup_d.rearrange("(a n) -> a n", a=1).to_broadcast([P, 2 * D]))),
            ("ld_o", lambda: (stage_o[:, :, :], wo_d.rearrange("(c p) n -> p c n", p=P))),
            ("ld_bo", lambda: (b_o[:, :], bo_d.rearrange("(a n) -> a n", a=1).to_broadcast([P, D]))),
            ("ld_bg", lambda: (b_g[:, :], bg_d.rearrange("(a n) -> a n", a=1).to_broadcast([P, E]))),
        ]
        for name, ops in loads:
            w(name, "act", [], lambda e, b, ops=ops: e.dma_start(*ops()), dma=True)
        w("ld_g", "act", ["W.zero_g"], lambda e, b: e.dma_start(
            stage_g[:, :, 0:E], wg_d.rearrange("(c p) n -> p c n", p=P)), dma=True)
        for c in range(C):
            w(f"ld_e{c}", "act", [], lambda e, b, c=c: e.dma_start(
                stage[:, c * E * D:(c + 1) * E * D].rearrange("p (e f) -> p e f", e=E),
                we_d[:, c * P:(c + 1) * P, :].rearrange("e p f -> p e f")), dma=True)
        for h in range(8):
            w(f"ld_f{h}", "act", ["W.zero_f"], lambda e, b, h=h: e.dma_start(
                stage_f[HD * h:HD * h + HD, h // 2, M * (h % 2):M * (h % 2) + M], rf_d), dma=True)

        def split(name, hi, lo, src, waits):
            w(name + "_hi", "dve", waits, lambda e, b: e.tensor_copy(hi, src))
            w(name + "_lo", "dve", [f"W.{name}_hi"], lambda e, b: e.tensor_tensor(
                lo, src, hi.bitcast(F32), ALU.subtract))

        def sel_tok_run(e, b):
            v = ident[:, :].rearrange("p (a t k) -> p t a k", t=2, k=HD)
            return e.tensor_reduce(sel_tok[:, :], v, AX.XY, ALU.add)

        w("sel_tok", "dve", ["W.ident"], sel_tok_run)
        w("tanh", "act", ["W.ld_gx", "W.ld_gf"], lambda e, b: (
            e.activation(tanh_x[:, :], g_cols[:, 0:1], ACT.Tanh),
            e.activation(tanh_f[:, :], g_cols[:, 1:2], ACT.Tanh))[1])
        w("f_scale", "dve", [f"W.ld_f{h}" for h in range(8)], lambda e, b: e.tensor_scalar(
            stage_f[:, :, :], stage_f[:, :, :], QK_SCALE, None, ALU.mult))
        split("wf", wf_hi[:, :, :], wf_lo[:, :, :], stage_f[:, :, :], ["W.f_scale"])

        def by_gamma(tile, gamma):
            def run(e, b):
                for c in range(C):
                    last = e.tensor_scalar(tile(c), tile(c), gamma[:, c:c + 1], None, ALU.mult)
                return last
            return run

        w("q_gamma", "dve", ["W.ld_q", "W.ld_g1"], lambda e, b: [
            e.tensor_scalar(qkv32[:, c, 0:D], stage_q[:, c, :], gamma1[:, c:c + 1], None, ALU.mult)
            for c in range(C)][-1])
        w("d_gamma", "dve", ["W.ld_dn", "W.ld_g1"], by_gamma(lambda c: stage_d[:, c, :], gamma1))
        w("g_gamma", "dve", ["W.ld_g", "W.ld_g2"], by_gamma(lambda c: stage_g[:, c, :], gamma2))
        w("e_gamma", "dve", ["W.ld_e0", "W.ld_e1", "W.ld_g2"],
          by_gamma(lambda c: stage[:, c * E * D:(c + 1) * E * D], gamma2))
        w("bdn_wide", "dve", ["W.ld_bdn"], lambda e, b: e.tensor_copy(
            bdn_wide[:, :], bdn_col[:, 0:1].to_broadcast([R, P])))
        w("dn_t", "pe", ["W.d_gamma", "W.ident"], lambda e, b: [
            e.transpose(f_ps[0:R, c, 0:P], stage_d[:, c, :], ident[:, :]) for c in range(C)][-1])
        w("dn_t_sb", "dve", ["W.dn_t"], lambda e, b: e.tensor_copy(wdn_t[:, :, :], f_ps[0:R, 0:C, 0:P]))
        w("kv", "pe", ["W.dn_t_sb", "W.ld_up"], lambda e, b: [
            e.matmul(f_ps[:, c, :], wdn_t[:, c, :], stage_u[:, :], start=True, stop=True)
            for c in range(C)][-1])
        w("bkv", "pe", ["W.bdn_wide", "W.ld_up"], lambda e, b: e.matmul(
            f_ps[:, C, :], bdn_wide[:, :], stage_u[:, :], start=True, stop=True))

        def kv_sb(e, b):
            for c in range(C):
                for s in range(2):
                    last = e.tensor_copy(
                        qkv32[:, c, D * (1 + s):D * (2 + s)].rearrange("p (g d) -> p g d", d=HD),
                        f_ps[:, c, :].rearrange("p (g s d) -> p s g d", s=2, d=HD)[:, s])
            return last

        w("kv_sb", "dve", ["W.kv"], kv_sb)
        w("bkv_sum", "dve", ["W.bkv", "W.ld_bup"], lambda e, b: e.tensor_tensor(
            stage_o2[:, :], f_ps[:, C, :], b_qkv[:, D:3 * D], ALU.add))
        w("bkv_sb", "dve", ["W.bkv_sum"], lambda e, b: [
            e.tensor_copy(b_qkv[:, D * (1 + s):D * (2 + s)].rearrange("p (g d) -> p g d", d=HD),
                          stage_o2[:, :].rearrange("p (g s d) -> p s g d", s=2, d=HD)[:, s])
            for s in range(2)][-1])
        split("wqkv", wqkv_hi[:, :, :], wqkv_lo[:, :, :], qkv32[:, :, :], ["W.kv_sb", "W.q_gamma"])
        split("wo", wo_hi[:, :, :], wo_lo[:, :, :], stage_o[:, :, :], ["W.ld_o"])
        split("wg", wg_hi[:, :, :], wg_lo[:, :, :], stage_g[:, :, :], ["W.g_gamma"])
        split("we", we_hi[:, :, :].rearrange("p a b -> p (a b)"),
              we_lo[:, :, :].rearrange("p a b -> p (a b)"), stage[:, :], ["W.e_gamma"])

        A = []
        A.append(Step("load", "sp", 100, ["A.square--"], lambda e, b: e.dma_start(
            c_chunk[b.par][:, :, :],
            ctx_d[bass.ds(b.times(CH), CH), :, :].rearrange("b (t p) d -> p (b t) d", p=P)), dma=True))
        A.append(Step("square", "act", 1900, ["A.load"], lambda e, b: e.activation(
            c_chunk[b.par][:, :, :], c_chunk[b.par][:, :, :], ACT.Square, scale=QK_SCALE)))
        A.append(Step("sum", "dve", 2200, ["A.square"], lambda e, b: e.tensor_reduce(
            hk[:, bass.ds(b.times(CH * T), CH * T), :],
            c_chunk[b.par][:, :, :].rearrange("p n (h d) -> p n h d", d=HD), AX.X, ALU.add)))
        A[0].waits = ["A.sum--"]

        S = []
        last_chunk = NB // CH - 1

        def s(name, eng, waits, run):
            S.append(Step(name, eng, 100, waits, run))

        s("min", "dve", ["A.end"], lambda e, b: e.tensor_reduce(
            hk_min[:, :], hk[:, :, :], AX.XY, ALU.min))
        s("col", "dve", ["S.min"], lambda e, b: e.tensor_scalar(
            hk_col[:, :], hk_min[:, :], -0.5, None, ALU.mult))
        s("stab", "pool", ["S.col"], lambda e, b: e.partition_all_reduce(
            stab[:, :], hk_col[:, :], P, bass.bass_isa.ReduceOp.max))
        s("less", "dve", ["S.stab"], lambda e, b: e.tensor_scalar(
            hk[:, :, :], hk[:, :, :], -0.5, stab[:, 0:1], ALU.mult, ALU.subtract))

        x_in = [sb(f"x_in{p}", [P, T, D]) for p in range(2)]
        c_in = [sb(f"c_in{p}", [P, T, D]) for p in range(2)]
        x1 = [sb(f"x1_{p}", [P, T, D]) for p in range(2)]
        bn6, mv = sb("bn6", [P, T, 6]), sb("mv", [P, T, 2])
        var_e, rstd = sb("var_e", [P, T]), sb("rstd", [P, T])
        xn = sb("xn", [P, T, D])
        q_hi, q_lo = sb("q_hi", [P, C, L], F32R), sb("q_lo", [P, C, L], F32R)
        k_hi, k_lo = sb("k_hi", [P, C, L], F32R), sb("k_lo", [P, C, L], F32R)
        h2 = sb("h2", [P, T, R])
        h_t = sb("h_t", [R, L], F32R)
        v1 = sb("v1", [P, T, H, 32])
        qf, kf = sb("qf", [P, PAIRS, L]), sb("kf", [P, PAIRS, L])
        att = [sb(f"att{n}", [P, 4, 3 * P]) for n in range(2)]
        nt = sb("nt", [P, QUADS, L])
        den3 = sb("den3", [P, 3, T, H])
        o_x = sb("o_x", [P, T, D])

        Pn = []

        def p(name, eng, ns, waits, run, dma=False, kind=""):
            Pn.append(Step(name, eng, ns, waits, run, dma, kind))

        def rows(dram, b):
            return dram[bass.ds(b.times(1), 1), :, :].rearrange("b (t p) d -> p (b t) d", p=P)

        p("x_load", "sp", 50, ["P.x1--"], lambda e, b: e.dma_start(x_in[b.par][:, :, :], rows(x_d, b)), True)
        p("c_load", "sp", 50, ["P.x1--"],
          lambda e, b: e.dma_start(c_in[b.par][:, :, :], rows(ctx_d, b)), True)

        p("bn", "dve", 700, ["P.x_load", "P.bn_agg-"], lambda e, b: [
            e.bn_stats(bn6[:, t, :], x_in[b.par][:, t, :]) for t in range(T)][-1])
        p("bn_agg", "dve", 150, ["P.bn", "P.xn-"], lambda e, b: [
            e.bn_aggr(mv[:, t, :], bn6[:, t, :]) for t in range(T)][-1], kind="aggr")
        p("var_e", "dve", 70, ["P.bn_agg", "P.rstd-"], lambda e, b: e.tensor_scalar(
            var_e[:, :], mv[:, :, 1], LN_EPS, None, ALU.add))
        p("rstd", "pool", 300, ["P.var_e", "P.xn-", "W.half"], lambda e, b: e.tensor_tensor(
            rstd[:, :], var_e[:, :], neg_half[:, 0:T], ALU.pow))
        p("xn", "dve", 450, ["P.rstd", "P.x_t-"], lambda e, b: [
            e.tensor_scalar(xn[:, t, :], x_in[b.par][:, t, :], mv[:, t, 0:1], rstd[:, t:t + 1],
                            ALU.subtract, ALU.mult) for t in range(T)][-1])

        def turn(bank, src):
            def run(e, b):
                for c in range(C):
                    for t in range(T):
                        last = e.transpose(bank(c)[:, t * P:(t + 1) * P],
                                           src(b)[:, t, c * P:(c + 1) * P], ident[:, :])
                return last
            return run

        def h2_run(e, b):
            src = hk[:, bass.ds(b.times(T), T), :]
            return e.activation(h2[:, :, 0:H].bitcast(F32R), src, ACT.Copy)

        p("h_hi", "act", 250, ["S.zero_h2", "P.h_tr-", "P.h_lo-"], h2_run)
        p("h_lo", "dve", 120, ["P.h_hi"], lambda e, b: e.tensor_tensor(
            h2[:, :, 32:32 + H], hk[:, bass.ds(b.times(T), T), :], h2[:, :, 0:H], ALU.subtract))
        p("v1", "pool", 600, ["P.c_load", "P.av3-", "S.one_v1"], lambda e, b: e.tensor_copy(
            v1[:, :, :, 0:HD], c_in[b.par][:, :, :].rearrange("p t (h d) -> p t h d", d=HD)), kind="scalar")
        p("c_t", "pe", 500, ["P.c_load", "P.x1-", "W.ident"],
          turn(lambda c: n_ps[:, 1, c * L:(c + 1) * L], lambda b: c_in[b.par]))
        p("k_hi", "act", 620, ["P.c_t"], lambda e, b: e.activation(
            k_hi[:, :, :].rearrange("p a b -> p (a b)"), n_ps[:, 1, :], ACT.Copy))
        p("k_lo", "dve", 620, ["P.k_hi"], lambda e, b: e.tensor_tensor(
            k_lo[:, :, :].rearrange("p a b -> p (a b)"), n_ps[:, 1, :],
            k_hi[:, :, :].rearrange("p a b -> p (a b)").bitcast(F32), ALU.subtract))
        bank, free = P_BANKS["h_t"]
        p("h_tr", "pe", 250, ["P.h_lo", free], lambda e, b, bank=bank: [
            e.transpose(p_ps[0:R, bank, t * P:(t + 1) * P], h2[:, t, :], ident[:, :]) for t in range(T)][-1], kind="small")
        p("h_t", "act", 420, ["P.h_tr"], lambda e, b, bank=bank: e.activation(
            h_t[:, :], p_ps[0:R, bank, 0:L], ACT.Copy))
        p("x_t", "pe", 500, ["P.xn", "P.x1-"],
          turn(lambda c: n_ps[:, 0, c * L:(c + 1) * L], lambda b: xn))
        p("q_hi", "act", 620, ["P.x_t"], lambda e, b: e.activation(
            q_hi[:, :, :].rearrange("p a b -> p (a b)"), n_ps[:, 0, :], ACT.Copy))
        p("q_lo", "dve", 620, ["P.q_hi"], lambda e, b: e.tensor_tensor(
            q_lo[:, :, :].rearrange("p a b -> p (a b)"), n_ps[:, 0, :],
            q_hi[:, :, :].rearrange("p a b -> p (a b)").bitcast(F32), ALU.subtract))

        def features(src_hi, src_lo, n, bank, with_h):
            def run(e, b):
                for half in range(2):
                    pr = 2 * n + half
                    c, r = divmod(pr, 4)
                    ps = p_ps[:, bank, half * L:(half + 1) * L]
                    e.matmul(ps, wf_hi[:, r, :], src_hi[:, c, :], start=True, stop=False)
                    e.matmul(ps, wf_lo[:, r, :], src_hi[:, c, :], start=False, stop=False)
                    last = e.matmul(ps, wf_hi[:, r, :], src_lo[:, c, :], start=False, stop=not with_h)
                    if with_h:
                        last = e.matmul(ps, h_sel[:, pr, :], h_t[:, :], start=False, stop=True)
                return last
            return run

        for key, hi, lo, dst in (("k", k_hi, k_lo, kf), ("q", q_hi, q_lo, qf)):
            pass
        order = [("q", q_hi, q_lo, qf), ("k", k_hi, k_lo, kf)]
        for key, hi, lo, dst in order:
            for n in range(4):
                bank, free = P_BANKS[f"{key}_exp{n}"]
                waits = [f"P.{key}_lo", free] + (["P.h_t"] if key == "k" else [])
                p(f"{key}_mm{n}", "pe", 970 if key == "k" else 720, waits + ["W.wf_lo", "W.h_sel"],
                  features(hi, lo, n, bank, key == "k"))
                flat = dst[:, 2 * n:2 * n + 2, :].rearrange("p a b -> p (a b)")
                p(f"{key}_exp{n}", "act", 620, [f"P.{key}_mm{n}", "P.a_mm3-"],
                  lambda e, b, bank=bank, flat=flat: e.activation(flat, p_ps[:, bank, :], ACT.Exp))
                p(f"{key}f{n}", "pool", 600, [f"P.{key}_exp{n}"],
                  lambda e, b, flat=flat: e.tensor_scalar(flat, flat, KERNEL_EPS, 1.0, ALU.add, ALU.mult), kind="scalar")

        def head(q, j):
            return 8 * (q // 2) + 2 * j + q % 2

        def scores(q, banks):
            def run(e, b):
                for kind, (tk, tq) in enumerate(((0, 0), (0, 1), (1, 1))):
                    for j in range(4):
                        pr, half = divmod(head(q, j), 2)
                        rows_ = slice(M * half, M * half + M)
                        last = e.matmul(p_ps[:, banks[kind], j * P:(j + 1) * P],
                                        kf[rows_, pr, tk * P:(tk + 1) * P],
                                        qf[rows_, pr, tq * P:(tq + 1) * P], start=True, stop=True)
                return last
            return run

        def av(q):
            def run(e, b):
                bank, col = divmod(q * L, 512)
                for part in range(2):
                    for j in range(4):
                        h = head(q, j)
                        out = n_ps[32 * j:32 * j + 32, bank, col + part * P:col + L]
                        a = att[q % 2][:, j, 2 * part * P:2 * P + part * P]
                        last = e.matmul(out, v1[:, part, h, :], a, start=(part == 0), stop=(part == 1),
                                        skip_group_check=True, tile_position=(0, 32 * j))
                return last
            return run

        for q in range(QUADS):
            banks, frees = [], []
            for kind in ("diag0", "cross", "diag1"):
                bank, free = P_BANKS[f"a_{kind}{q}"]
                banks.append(bank)
                frees.append(free)
            p(f"a_mm{q}", "pe", 2750, frees + [f"P.qf{q | 1}", f"P.kf{q | 1}"], scores(q, banks))
            reader = f"P.av{q - 2}" if q >= 2 else f"P.av{q + 2}-"
            mask = causal[:, :].unsqueeze(1).to_broadcast([P, 4, P])

            def masked(q, bank, col):
                return lambda e, b: e.tensor_tensor(
                    att[q % 2][:, :, col:col + P],
                    p_ps[:, bank, :].rearrange("p (j l) -> p j l", j=4), mask, ALU.mult)

            p(f"a_diag0{q}", "dve", 620, [f"P.a_mm{q}", reader, "W.tri"], masked(q, banks[0], 0))
            p(f"a_cross{q}", "act", 620, [f"P.a_mm{q}", reader], lambda e, b, q=q, bank=banks[1]: e.activation(
                att[q % 2][:, :, P:2 * P], p_ps[:, bank, :].rearrange("p (j l) -> p j l", j=4), ACT.Copy))
            p(f"a_diag1{q}", "dve", 620, [f"P.a_mm{q}", reader], masked(q, banks[2], 2 * P))
            if q:
                p(f"av{q - 1}", "pe", 650, [f"P.a_diag1{q - 1}", f"P.a_cross{q - 1}", "P.v1", "P.q_lo", "P.k_lo"],
                  av(q - 1))
        p(f"av{QUADS - 1}", "pe", 650, [f"P.a_diag1{QUADS - 1}", f"P.a_cross{QUADS - 1}"], av(QUADS - 1))

        p("nt", "act", 1050, [f"P.av{QUADS - 1}", "P.nt_t-"], lambda e, b: e.activation(
            nt[:, :, :].rearrange("p a b -> p (a b)"), n_ps[:, :, :].rearrange("p a b -> p (a b)"), ACT.Copy))
        p("nt_t", "pe", 1000, ["P.nt"], lambda e, b: [
            e.transpose(n_ps[:, t, :].rearrange("p (a j s v) -> p a s j v", a=2, s=2, v=32)[:, q // 2, q % 2],
                        nt[:, q, t * P:(t + 1) * P], ident[:, :])
            for t in range(T) for q in range(QUADS)][-1])
        nd = n_ps[:, :, :].rearrange("p t (h v) -> p t h v", v=32)
        p("den_small", "dve", 100, ["P.nt_t", "P.den-"], lambda e, b: e.tensor_scalar(
            den3[:, 0], nd[:, :, :, HD], M * NORM_STAB, None, ALU.is_le))
        p("den", "dve", 100, ["P.den_small"], lambda e, b: e.scalar_tensor_tensor(
            out=den3[:, 1], in0=den3[:, 0], scalar=2.0 * M * NORM_STAB, in1=nd[:, :, :, HD],
            op0=ALU.mult, op1=ALU.add))
        p("recip", "dve", 100, ["P.den"], lambda e, b: e.reciprocal(den3[:, 2], den3[:, 1]))
        p("recip_g", "dve", 70, ["P.recip", "W.tanh"], lambda e, b: e.tensor_scalar(
            den3[:, 1], den3[:, 2], tanh_x[:, 0:1], None, ALU.mult))
        p("o_x", "dve", 620, ["P.recip_g"], lambda e, b: [e.tensor_tensor(
            o_x[:, t, :].rearrange("p (h d) -> p h d", d=HD), nd[:, t, :, 0:HD],
            den3[:, 1, t, :].unsqueeze(2).to_broadcast([P, H, HD]), ALU.mult) for t in range(T)][-1])
        p("x1", "dve", 620, ["P.o_x", "P.x_load", "F.out--"], lambda e, b: e.tensor_tensor(
            x1[b.par][:, :, :], o_x[:, :, :], x_in[b.par][:, :, :], ALU.add))

        s("zero_h2", "dve", [], lambda e, b: e.memset(h2[:, :, :], 0.0))
        s("zero_v1", "dve", [], lambda e, b: e.memset(v1[:, :, :, :], 0.0))
        s("one_v1", "dve", ["S.zero_v1"], lambda e, b: e.memset(v1[:, :, :, HD:HD + 1], 1.0))

        Fn = []
        def f(name, eng, ns, waits, run, dma=False, kind=""):
            Fn.append(Step(name, eng, ns, waits, run, dma, kind))

        f("bn", "dve", 700, ["P.x1", "F.bn_agg-"], lambda e, b: [
            e.bn_stats(bn6f[:, t, :], x1[b.par][:, t, :]) for t in range(T)][-1])
        f("bn_agg", "dve", 150, ["F.bn", "F.hn-"], lambda e, b: [
            e.bn_aggr(mvf[:, t, :], bn6f[:, t, :]) for t in range(T)][-1], kind="aggr")
        f("var", "dve", 140, ["F.bn_agg", "F.rstd-"], lambda e, b: (
            e.tensor_scalar(var_f[:, 0, :], mvf[:, :, 1], LN_EPS, None, ALU.add),
            e.tensor_scalar(var_f[:, 1, :], mvf[:, :, 1], 1.0 + RMS_EPS, RMS_EPS * LN_EPS,
                            ALU.mult, ALU.add))[1])
        f("rstd", "pool", 300, ["F.var", "F.hn-"], lambda e, b: e.tensor_tensor(
            r_f[:, :, :].rearrange("p a b -> p (a b)"), var_f[:, :, :].rearrange("p a b -> p (a b)"),
            neg_half[:, 0:2 * T], ALU.pow))
        def norm(dst, which):
            return lambda e, b: [e.tensor_scalar(
                dst[:, t, :], x1[b.par][:, t, :], mvf[:, t, 0:1], r_f[:, which, t:t + 1],
                ALU.subtract, ALU.mult) for t in range(T)][-1]
        f("hn", "dve", 450, ["F.rstd", "F.h_t1-"], norm(hn, 1))
        f("y", "dve", 450, ["F.rstd", "F.yb-"], norm(y, 0))
        A_bo = b_o[:, :].unsqueeze(1).to_broadcast([P, T, D])
        f("yb", "pool", 1200, ["F.y", "F.y2-", "W.ld_bo"], lambda e, b: e.tensor_tensor(
            yb[:, :, :], y[:, :, :], A_bo, ALU.add))

        def turn_c(name, src, waits, hi, lo, readers):
            for c in range(C):
                bank, free = F_BANKS[f"{readers}{c}"]
                f(f"{name}{c}", "pe", 250, waits + [free], lambda e, b, c=c, bank=bank: [
                    e.transpose(f_ps[:, bank, t * P:(t + 1) * P], src[:, t, c * P:(c + 1) * P],
                                ident[:, :]) for t in range(T)][-1])
                f(f"{name}_hi{c}", "act", 400, [f"F.{name}{c}"], lambda e, b, c=c, bank=bank:
                  e.activation(hi[:, c, :], f_ps[:, bank, 0:L], ACT.Copy))
                f(f"{readers}{c}", "dve", 380, [f"F.{name}_hi{c}"], lambda e, b, c=c, bank=bank:
                  e.tensor_tensor(lo[:, c, :], f_ps[:, bank, 0:L], hi[:, c, :].bitcast(F32), ALU.subtract))

        turn_c("h_t", hn, ["F.hn"], ht_hi, ht_lo, "ht_lo")

        def three_passes(e, out, a_hi, a_lo, b_hi, b_lo):
            for c in range(C):
                e.matmul(out, a_hi(c), b_hi(c), start=(c == 0), stop=False)
                e.matmul(out, a_hi(c), b_lo(c), start=False, stop=False)
                last = e.matmul(out, a_lo(c), b_hi(c), start=False, stop=(c == C - 1))
            return last

        def tok(tile, t):
            return lambda c: tile[:, c, t * P:(t + 1) * P]

        def cols(tile, a, b_):
            return lambda c: tile[:, c, a:b_]

        for t in range(T):
            bank, free = F_BANKS[f"qk{t}"]
            f(f"qk_mm{t}", "pe", 1370, ["F.ht_lo1", free, "W.wqkv_lo"], lambda e, b, t=t, bank=bank: three_passes(
                e, f_ps[:, bank, :], tok(ht_hi, t), tok(ht_lo, t),
                cols(wqkv_hi, 0, 2 * D), cols(wqkv_lo, 0, 2 * D)))
            f(f"qk{t}", "dve", 620, [f"F.qk_mm{t}", "F.k_t-", "W.bkv_sb", "W.ld_bq"], lambda e, b, t=t, bank=bank:
              e.tensor_tensor(qkv[:, t, 0:2 * D], f_ps[:, bank, :], b_qkv[:, 0:2 * D], ALU.add))
        bank, free = F_BANKS["vv"]

        def v_mm(e, b, bank=bank):
            for t in range(T):
                last = three_passes(e, f_ps[:, bank, t * D:(t + 1) * D], tok(ht_hi, t), tok(ht_lo, t),
                                    cols(wqkv_hi, 2 * D, 3 * D), cols(wqkv_lo, 2 * D, 3 * D))
            return last

        f("v_mm", "pe", 1440, [free], v_mm)
        f("vv", "dve", 620, ["F.v_mm", "F.v_t-"], lambda e, b, bank=bank: e.tensor_tensor(
            qkv[:, :, 2 * D:3 * D], f_ps[:, bank, :].rearrange("p (t n) -> p t n", t=T),
            b_qkv[:, 2 * D:3 * D].unsqueeze(1).to_broadcast([P, T, D]), ALU.add))

        def heads_of(a):
            return qkv[:, :, a:a + D].rearrange("p t (h d) -> p h t d", d=HD)

        f("q_t", "dve", 620, ["F.qk1", "F.q_bd-"], lambda e, b: e.transpose(q_t[:, :, :], heads_of(0)))
        f("q_bd", "dve", 650, ["F.q_t", "F.s_mm-", "W.sel_tok"], lambda e, b: [e.tensor_scalar(
            q_bd[:, t, :, :], q_t[:, :, :], sel_tok[:, t:t + 1], None, ALU.mult) for t in range(T)][-1])
        f("k_t", "dve", 620, ["F.qk1", "F.s_mm-"], lambda e, b: e.transpose(k_t[:, :, :], heads_of(D)))

        bank, free = F_BANKS["s_sub"]

        def s_mm(e, b, bank=bank):
            for n in range(32):
                for j in range(4):
                    r = slice(32 * j, 32 * j + 32)
                    last = e.matmul(f_ps[r, bank, n * H:(n + 1) * H], q_bd[r, :, :, n], k_t[r, :, n],
                                    start=True, stop=True, tile_position=(32 * j, 32 * j))
            return last

        f("s_mm", "pe", 8700, ["F.q_bd", "F.k_t", free], s_mm, kind="small")
        f("v_t", "dve", 620, ["F.vv", "F.pv-"], lambda e, b: e.transpose(
            v_t[:, :, :], qkv[:, :, 2 * D:3 * D].rearrange("p t (g d) -> p d t g", d=HD)))
        sc = f_ps[:, bank, :].rearrange("p (n g) -> p n g", g=H)

        def per_row(tile):
            return tile[:, :].unsqueeze(2).to_broadcast([P, 32, H])

        f("s_max", "dve", 620, ["F.s_mm", "F.s_sub-"], lambda e, b: e.tensor_reduce(
            s_max[:, :], sc, AX.X, ALU.max))
        f("s_sub", "dve", 620, ["F.s_max", "F.s_exp-"], lambda e, b: e.tensor_tensor(
            s_sub[:, :, :], sc, per_row(s_max), ALU.subtract))
        f("s_exp", "act", 620, ["F.s_sub", "F.s_norm-"], lambda e, b: e.activation(
            s_exp[:, :, :], s_sub[:, :, :], ACT.Exp, scale=float(HD) ** -0.5))
        f("s_sum", "dve", 620, ["F.s_exp"], lambda e, b: e.tensor_reduce(
            s_sum[:, :], s_exp[:, :, :], AX.X, ALU.add))
        f("s_rec", "dve", 90, ["F.s_sum"], lambda e, b: e.reciprocal(s_rec[:, :], s_sum[:, :]))
        f("s_norm", "dve", 620, ["F.s_rec"], lambda e, b: e.tensor_tensor(
            s_exp[:, :, :], s_exp[:, :, :], per_row(s_rec), ALU.mult))
        f("p_bd", "dve", 650, ["F.s_norm"], lambda e, b: [e.tensor_scalar(
            p_bd[:, :, t, :], s_exp[:, :, :], sel_tok[:, t:t + 1], None, ALU.mult) for t in range(T)][-1])
        f("p_t", "dve", 1150, ["F.p_bd", "F.pv-"], lambda e, b: e.transpose(
            p_t[:, :, :], p_bd[:, :, :, :].rearrange("p n t g -> p n (t g)")))
        bank, free = F_BANKS["o_tok"]

        def pv(e, b, bank=bank):
            for n in range(32):
                for j in range(4):
                    r = slice(32 * j, 32 * j + 32)
                    last = e.matmul(f_ps[r, bank, n * HD:(n + 1) * HD], p_t[r, n, :], v_t[r, :, n],
                                    start=True, stop=True, tile_position=(32 * j, 32 * j))
            return last

        f("pv", "pe", 8700, ["F.p_t", "F.v_t", free], pv, kind="small")
        f("o_tok", "dve", 620, ["F.pv", "F.o_tr-"], lambda e, b, bank=bank: e.transpose(
            o_tok[:, :, :].rearrange("p t (h d) -> p d t h", d=HD),
            f_ps[:, bank, :].rearrange("p (n d) -> p d n", d=HD)))

        bank, free = F_BANKS["ot_lo"]
        f("o_tr", "pe", 500, ["F.o_tok", free], lambda e, b, bank=bank: [
            e.transpose(f_ps[:, bank, c * L + t * P:c * L + (t + 1) * P], o_tok[:, t, c * P:(c + 1) * P],
                        ident[:, :]) for c in range(C) for t in range(T)][-1])
        f("ot_hi", "act", 620, ["F.o_tr"], lambda e, b, bank=bank: e.activation(
            ot_hi[:, :, :].rearrange("p a b -> p (a b)"), f_ps[:, bank, :], ACT.Copy))
        f("ot_lo", "dve", 620, ["F.ot_hi"], lambda e, b, bank=bank: e.tensor_tensor(
            ot_lo[:, :, :].rearrange("p a b -> p (a b)"), f_ps[:, bank, :],
            ot_hi[:, :, :].rearrange("p a b -> p (a b)").bitcast(F32), ALU.subtract))
        bank, free = F_BANKS["y2"]

        def o_mm(e, b, bank=bank):
            for t in range(T):
                last = three_passes(e, f_ps[:, bank, t * D:(t + 1) * D], tok(ot_hi, t), tok(ot_lo, t),
                                    cols(wo_hi, 0, D), cols(wo_lo, 0, D))
            return last

        f("o_mm", "pe", 1440, ["F.ot_lo", free, "W.wo_lo"], o_mm)
        f("y2", "dve", 620, ["F.o_mm", "F.yb", "F.e0_0a-", "F.e1_0a-", "F.h2n-"], lambda e, b, bank=bank:
          e.tensor_tensor(y2[:, :, :], f_ps[:, bank, :].rearrange("p (t n) -> p t n", t=T),
                          yb[:, :, :], ALU.add))
        f("bn2", "dve", 700, ["F.y2", "F.hn"], lambda e, b: [
            e.bn_stats(bn6f[:, t, :], y2[:, t, :]) for t in range(T)][-1])
        f("bn2_agg", "dve", 150, ["F.bn2", "F.y"], lambda e, b: [
            e.bn_aggr(mvf[:, t, :], bn6f[:, t, :]) for t in range(T)][-1], kind="aggr")
        f("ms0", "dve", 70, ["F.bn2_agg", "F.ms-"], lambda e, b: e.tensor_tensor(
            ms[:, :], mvf[:, :, 0], mvf[:, :, 0], ALU.mult))
        f("ms1", "dve", 70, ["F.ms0", "F.r2-"], lambda e, b: e.tensor_tensor(
            gm[:, :], ms[:, :], mvf[:, :, 1], ALU.add))
        f("ms", "dve", 70, ["F.ms1"], lambda e, b: e.tensor_scalar(
            ms[:, :], gm[:, :], RMS_EPS, None, ALU.add))
        f("r2", "pool", 300, ["F.ms", "F.h2n-"], lambda e, b: e.tensor_tensor(
            r2[:, :], ms[:, :], neg_half[:, 0:T], ALU.pow))
        f("h2n", "dve", 450, ["F.r2", "F.h2_t1-"], lambda e, b: [e.tensor_scalar(
            h2n[:, t, :], y2[:, t, :], r2[:, t:t + 1], None, ALU.mult) for t in range(T)][-1])
        turn_c("h2_t", h2n, ["F.h2n"], h2_hi, h2_lo, "h2_lo")

        bank, free = F_BANKS["gl"]
        f("g_mm", "pe", 730, ["F.h2_lo1", free, "W.wg_lo"], lambda e, b, bank=bank: three_passes(
            e, f_ps[:, bank, 0:L], lambda c: wg_hi[:, c, :], lambda c: wg_lo[:, c, :],
            lambda c: h2_hi[:, c, :], lambda c: h2_lo[:, c, :]))
        f("gl", "act", 420, ["F.g_mm", "F.g_t-"], lambda e, b, bank=bank: e.activation(
            gl[:, :], f_ps[0:E, bank, 0:L], ACT.Copy))
        gbank, gfree = F_BANKS["ga"]

        def g_steps():
            bank, free = gbank, gfree
            f("g_t", "pe", 150, ["F.gl", free], lambda e, b, bank=bank: [
                e.transpose(f_ps[:, bank, t * E:(t + 1) * E], gl[:, t * P:(t + 1) * P], ident[0:E, 0:E])
                for t in range(T)][-1], kind="small")
            f("ga", "dve", 90, ["F.g_t", "F.gb-", "W.ld_bg"], lambda e, b, bank=bank: e.tensor_tensor(
                ga[:, :, :], f_ps[:, bank, 0:T * E].rearrange("p (t e) -> p t e", t=T),
                b_g[:, :].unsqueeze(1).to_broadcast([P, T, E]), ALU.add))
            f("gmax", "dve", 90, ["F.ga", "F.ms"], lambda e, b: e.tensor_reduce(gm[:, :], ga[:, :, :], AX.X, ALU.max))
            f("gb", "dve", 90, ["F.gmax", "F.gexp-"], lambda e, b: e.tensor_tensor(
                gb[:, :, :], ga[:, :, :], gm[:, :].unsqueeze(2).to_broadcast([P, T, E]), ALU.subtract))
            f("gexp", "act", 250, ["F.gb", "F.e1_3b-"], lambda e, b: e.activation(
                gate[:, :, :], gb[:, :, :], ACT.Exp))
            f("gsum", "dve", 90, ["F.gexp"], lambda e, b: e.tensor_reduce(gm[:, :], gate[:, :, :], AX.X, ALU.add))
            f("grec", "dve", 90, ["F.gsum"], lambda e, b: e.reciprocal(gr[:, :], gm[:, :]))
            f("gate", "dve", 90, ["F.grec"], lambda e, b: e.tensor_tensor(
                gate[:, :, :], gate[:, :, :], gr[:, :].unsqueeze(2).to_broadcast([P, T, E]), ALU.mult))

        g_steps()

        for t in range(T):
            for n in range(4):
                bank, free = F_BANKS[f"e{t}_{n}b"]
                f(f"e_mm{t}_{n}", "pe", 1370, ["F.h2_lo1", free, "W.we_lo"], lambda e, b, t=t, n=n, bank=bank:
                  three_passes(e, f_ps[:, bank, :], tok(h2_hi, t), tok(h2_lo, t),
                               cols(we_hi, 2 * n * D, 2 * (n + 1) * D), cols(we_lo, 2 * n * D, 2 * (n + 1) * D)))
                for half in range(2):
                    ex = 2 * n + half
                    src = y2[:, t, :] if ex == 0 else acc[t][(ex - 1) % 2][:, :]
                    before = "F.gate" if ex == 0 else f"F.e{t}_{(ex - 1) // 2}{'ab'[(ex - 1) % 2]}"
                    waits = [f"F.e_mm{t}_{n}", before] + (["F.out-"] if ex == 1 else [])
                    f(f"e{t}_{n}{'ab'[half]}", "dve", 350, waits, lambda e, b, t=t, ex=ex, half=half, bank=bank, src=src:
                      e.scalar_tensor_tensor(out=acc[t][ex % 2][:, :], in0=f_ps[:, bank, half * D:(half + 1) * D],
                                             scalar=gate[:, t, ex:ex + 1], in1=src, op0=ALU.mult, op1=ALU.add))
        f("out", "dve", 700, ["F.e0_3b", "F.e1_3b", "F.store--", "W.tanh"], lambda e, b: [
            e.scalar_tensor_tensor(out=outb[b.par][:, t, :], in0=acc[t][1][:, :], scalar=tanh_f[:, 0:1],
                                   in1=x1[b.par][:, t, :], op0=ALU.mult, op1=ALU.add) for t in range(T)][-1])
        f("store", "sp", 50, ["F.out"], lambda e, b: e.dma_start(
            out_d[bass.ds(b.times(1), 1), :, :].rearrange("b (t p) d -> p (b t) d", p=P),
            outb[b.par][:, :, :]), True)

        for key, steps in (("W", W), ("A", A), ("S", S), ("P", Pn), ("F", Fn)):
            streams[key] = Stream(key, steps, sem)

        names = {"pe": "tensor", "act": "scalar", "dve": "vector", "pool": "gpsimd", "sp": "sync"}
        both = merged([("P", Pn), ("F", Fn)])

        def emit(eng_key, eng, key, steps, batch):
            for st in steps:
                if st.eng == eng_key:
                    streams[key].emit(st, eng, batch, streams)

        def first(st):
            return st.dma or st.eng == "pool" or st.name.startswith("zero")

        def program(eng_key, eng):
            emit(eng_key, eng, "W", [st for st in W if first(st)], Batch(0, 0))
            for k in range(2):
                emit(eng_key, eng, "A", A, Batch(0, k))
            if eng_key in ("sp", "act", "dve"):
                with eng.Fori(1, NB // CH // 2) as i:
                    for k in range(2):
                        emit(eng_key, eng, "A", A, Batch(i, k))
            emit(eng_key, eng, "W", [st for st in W if not first(st)], Batch(0, 0))
            emit(eng_key, eng, "S", S, Batch(0, 0))

            def beside(i, k):
                for key, st in both:
                    if st.eng == eng_key:
                        streams[key].emit(st, eng, Batch(i, k) if key == "P" else Batch(i, k - 1), streams)

            emit(eng_key, eng, "P", Pn, Batch(0, 0))
            beside(0, 1)
            with eng.Fori(0, (NB - 2) // 2) as i:
                beside(i, 2)
                beside(i, 3)
            emit(eng_key, eng, "F", Fn, Batch((NB - 2) // 2, 1))
            if eng_key == "sp":
                for par in range(2):
                    st_sem, per_i, value = streams["F"].target("store", Batch(0, par))
                    eng.wait_ge(st_sem, (NB - 2) // 2 * per_i + value)

        streams["A"].place["end"] = streams["A"].place["sum"]
        end_steps = Step("end", "dve", 0, [], None)
        streams["A"].by_name["end"] = end_steps
        plain = streams["A"].target

        def a_target(name, batch):
            if name != "end":
                return plain(name, batch)
            sem_, _, value = plain("sum", Batch(0, last_chunk))
            return sem_, 0, value

        streams["A"].target = a_target

        block = ctx.enter_context(nc.Block())

        @block.sync
        def _(eng):
            program("sp", eng)

        @block.gpsimd
        def _(eng):
            program("pool", eng)

        @block.scalar
        def _(eng):
            program("act", eng)

        @block.vector
        def _(eng):
            program("dve", eng)

        @block.tensor
        def _(eng):
            program("pe", eng)


_INS = ['x', 'ctx_1024', 'g_xattn', 'g_ffn', 'L0_xattn_random_features', 'L0_ffn_gamma1', 'L0_ffn_Wq',
        'L0_ffn_bq', 'L0_ffn_Wdown', 'L0_ffn_bdown', 'L0_ffn_Wup', 'L0_ffn_bup', 'L0_ffn_Wo', 'L0_ffn_bo',
        'L0_ffn_gamma2', 'L0_ffn_Wg', 'L0_ffn_bg', 'L0_ffn_We']


def kernel(**inputs):
    import numpy as _np
    import concourse.bacc as _bacc
    from concourse import mybir as _mybir
    from concourse.bass_utils import run_bass_kernel_spmd as _run

    nc = _bacc.Bacc("TRN2", target_bir_lowering=False, num_devices=1)
    arrays, args = {}, []
    for name in _INS:
        a = _np.ascontiguousarray(inputs[name])
        arrays[f"in_{name}"] = a
        args.append(nc.dram_tensor(f"in_{name}", a.shape, _mybir.dt.from_np(a.dtype), kind="ExternalInput").ap())
    args.append(nc.dram_tensor("out_0", (NB, L, D), F32, kind="ExternalOutput").ap())
    build(nc, *args)
    r = _run(nc, [arrays], core_ids=[0])
    return r.results[0]["out_0"]
```

```python
from contextlib import ExitStack

import concourse.bass as bass
from concourse import mybir

F32 = mybir.dt.float32
F32R = mybir.dt.float32r
ALU = mybir.AluOpType
ACT = mybir.ActivationFunctionType
AX = mybir.AxisListType

P = 128
NB, L, D = 32, 256, 256
T = L // P
C = D // P
H, HD = 16, 16
M = 64
PAIRS = H * M // P
QUADS = H // 4
PARTS = 4
E = 8
R = 64
KERNEL_EPS, NORM_STAB = 1e-4, 1e-6
LN_EPS, RMS_EPS = 1e-5, 1e-6
QK_SCALE = D ** -0.25
CH = 4


SEPARATE_WAIT = {("dve", "aggr"), ("pe", "small"), ("pool", "scalar"), ("sp", "")}


BATCHED = "AQPGF"
FAR = 10 ** 9
PREFER = {'Q': 1511, 'F': -118}
TOL = 0
SCALE = {'qk_mm': 1.2, 'k_exp': 0.85, 'x_load': 0.85}


class Step:

    def __init__(self, name, eng, ns, waits, run, dma=False, kind=""):
        self.name, self.eng, self.ns, self.waits, self.run, self.dma = name, eng, ns, waits, run, dma
        self.kind = kind


class Batch:

    def __init__(self, i, k):
        self.i, self.k, self.par = i, k, k % 2

    def times(self, c, add=0):
        return self.i * (2 * c) + (self.k * c + add)

    def before(self, n):
        return Batch(self.i, self.k - n)

    def is_before_first(self, n):
        return isinstance(self.i, int) and 2 * self.i + self.k - n < 0


class Stream:

    def __init__(self, key, steps, new_sem):
        self.key, self.steps = key, steps
        self.per_batch, self.place, self.sems = {}, {}, {}
        for s in steps:
            if s.dma:
                self.sems[s.name] = [new_sem(f"{key}_{s.name}_{p}") for p in range(2)]
                continue
            self.per_batch[s.eng] = self.per_batch.get(s.eng, 0) + 1
            self.place[s.name] = self.per_batch[s.eng]
            if s.eng not in self.sems:
                self.sems[s.eng] = new_sem(f"{key}_{s.eng}")
        self.by_name = {s.name: s for s in steps}

    def target(self, name, batch):
        s = self.by_name[name]
        if s.dma:
            return self.sems[name][batch.par], 16, (batch.k // 2 + 1) * 16
        c = self.per_batch[s.eng]
        return self.sems[s.eng], 2 * c, batch.k * c + self.place[name]

    def emit(self, step, eng, batch, streams):
        needed = {}
        for w in step.waits:
            name = w.rstrip("-")
            back = len(w) - len(name)
            key, name = name.split(".")
            at = batch if key in BATCHED else Batch(0, 0)
            if at.is_before_first(back):
                continue
            sem, per_i, value = streams[key].target(name, at.before(back))
            per_i = per_i if key in BATCHED else 0
            if sem.name not in needed or needed[sem.name][2] < value:
                needed[sem.name] = (sem, per_i, value)
        waited = False
        for sem, per_i, value in needed.values():
            if waited and step.eng == "sp":
                eng.nop(nofuse=True)
            eng.wait_ge(sem, batch.i * per_i + value if per_i else value)
            waited = waited or bool(per_i) and not isinstance(batch.i, int)
        if waited and (step.eng, step.kind) in SEPARATE_WAIT:
            eng.nop(nofuse=True)
        last = step.run(eng, batch)
        if step.dma:
            last.then_inc(self.sems[step.name][batch.par], 16)
        else:
            last.then_inc(self.sems[step.eng], 1)


def merged(lists):
    ahead = {key: n for key, n, _ in lists}
    free, done, order = {}, {}, []
    taken = {key: 0 for key in ahead}
    heads = [0] * len(lists)
    while any(h < len(l) for h, (_, _, l) in zip(heads, lists)):
        best = None
        for n, (key, off, l) in enumerate(lists):
            if heads[n] == len(l):
                continue
            s = l[heads[n]]
            start = free.get(s.eng, 0)
            for w in s.waits:
                name = w.rstrip("-")
                if name[0] in ahead and off - (len(w) - len(name)) == ahead[name[0]]:
                    start = max(start, done.get(name, FAR))
            rank = start + PREFER.get(key, 0)
            if best is None or rank < best[0] or rank <= best[0] + TOL and taken[key] < taken[best[3]]:
                best = (rank, start, n, key, s)
        _, start, n, key, s = best
        assert start < FAR, s.name
        heads[n] += 1
        ns = s.ns * SCALE.get(s.name.rstrip("0123"), 1)
        free[s.eng] = start + ns
        taken[key] += s.ns if s.eng == "pe" else 0
        done[f"{key}.{s.name}"] = start + ns + 150
        order.append((key, s))
    return order


P_BANKS = {
    "h_t": (0, "P.a_diag03-"), "q_exp0": (1, "P.a_cross3-"), "q_exp1": (2, "P.a_diag13-"),
    "q_exp2": (0, "P.h_t"), "q_exp3": (1, "P.q_exp0"), "k_exp0": (2, "P.q_exp1"),
    "k_exp1": (0, "P.q_exp2"), "k_exp2": (1, "P.q_exp3"), "k_exp3": (2, "P.k_exp0"),
    "a_diag00": (0, "P.k_exp1"), "a_cross0": (1, "P.k_exp2"), "a_diag10": (2, "P.k_exp3"),
    "a_diag01": (0, "P.a_diag00"), "a_cross1": (1, "P.a_cross0"), "a_diag11": (2, "P.a_diag10"),
    "a_diag02": (0, "P.a_diag01"), "a_cross2": (1, "P.a_cross1"), "a_diag12": (2, "P.a_diag11"),
    "a_diag03": (0, "P.a_diag02"), "a_cross3": (1, "P.a_cross2"), "a_diag13": (2, "P.a_diag12"),
}
F_BANKS = {
    "qk0": (0, "F.e1_1b-"), "qk1": (1, "F.e1_2b-"), "vv": (2, "F.e1_3b-"),
    "s_sub": (0, "F.qk0"), "o_tok": (1, "F.qk1"), "ot_lo": (2, "F.vv"),
    "y2": (0, "F.s_sub"), "h2_lo0": (1, "F.o_tok"), "h2_lo1": (2, "F.ot_lo"),
    "ga": (0, "F.y2"), "e0_0b": (1, "F.h2_lo0"), "e0_1b": (2, "F.h2_lo1"),
    "e0_2b": (0, "F.ga"), "e0_3b": (1, "F.e0_0b"), "e1_0b": (2, "F.e0_1b"),
    "e1_1b": (0, "F.e0_2b"), "e1_2b": (1, "F.e0_3b"), "e1_3b": (2, "F.e1_0b"),
}


def build(nc, x_d, ctx_d, gx_d, gf_d, rf_d, g1_d, wq_d, bq_d, wdn_d, bdn_d, wup_d, bup_d,
          wo_d, bo_d, g2_d, wg_d, bg_d, we_d, out_d):
    ctx = ExitStack()
    with ctx:
        def sb(name, shape, dt=F32):
            return ctx.enter_context(nc.sbuf_tensor(name, shape, dt))

        def sem(name):
            return ctx.enter_context(nc.semaphore(name))

        ctx.enter_context(nc.allow_non_contiguous_dma(reason="a few small parameter vectors"))

        p_ps = ctx.enter_context(nc.psum_tensor("p_ps", [P, 3, 512], F32))
        n_ps = ctx.enter_context(nc.psum_tensor("n_ps", [P, 2, 512], F32))
        f_ps = ctx.enter_context(nc.psum_tensor("f_ps", [P, 3, 512], F32))

        ident = sb("ident", [P, P])
        causal = sb("causal", [P, P])
        sel_tok = sb("sel_tok", [P, 2])
        neg_half = sb("neg_half", [P, 4])
        wf_hi, wf_lo = sb("wf_hi", [P, 4, P], F32R), sb("wf_lo", [P, 4, P], F32R)
        h_sel = sb("h_sel", [R, PAIRS, P], F32R)
        wqkv_hi, wqkv_lo = sb("wqkv_hi", [P, C, 3 * D], F32R), sb("wqkv_lo", [P, C, 3 * D], F32R)
        wo_hi, wo_lo = sb("wo_hi", [P, C, D], F32R), sb("wo_lo", [P, C, D], F32R)
        wg_hi, wg_lo = sb("wg_hi", [P, C, P], F32R), sb("wg_lo", [P, C, P], F32R)
        we_hi, we_lo = sb("we_hi", [P, C, E * D], F32R), sb("we_lo", [P, C, E * D], F32R)
        b_qkv = sb("b_qkv", [P, 3 * D])
        b_o = sb("b_o", [P, D])
        b_g = sb("b_g", [P, E])
        tanh_x, tanh_f = sb("tanh_x", [P, 1]), sb("tanh_f", [P, 1])
        g_cols = sb("g_cols", [P, 2])
        hk = sb("hk", [P, NB * T, H])
        hk_min, hk_col, stab = sb("hk_min", [P, 1]), sb("hk_col", [P, 1]), sb("stab", [P, 1])

        streams = {}

        early = ExitStack()
        stage = early.enter_context(nc.sbuf_tensor("stage", [P, C * E * D], F32))
        c_chunk = [early.enter_context(nc.sbuf_tensor(f"c_chunk{p}", [P, CH * T, D], F32)) for p in range(2)]
        stage_q = early.enter_context(nc.sbuf_tensor("stage_q", [P, C, D], F32))
        stage_o = early.enter_context(nc.sbuf_tensor("stage_o", [P, C, D], F32))
        qkv32 = early.enter_context(nc.sbuf_tensor("qkv32", [P, C, 3 * D], F32))
        stage_o2 = early.enter_context(nc.sbuf_tensor("stage_o2", [P, 2 * D], F32))
        early.close()
        bn6f, mvf = sb("bn6f", [P, T, 6]), sb("mvf", [P, T, 2])
        bn6g, mvg = sb("bn6g", [P, T, 6]), sb("mvg", [P, T, 2])
        var_f, r_f = sb("var_f", [P, 2, T]), sb("r_f", [P, 2, T])
        y, yb, hn = sb("y", [P, T, D]), sb("yb", [P, T, D]), sb("hn", [P, T, D])
        ht_hi, ht_lo = sb("ht_hi", [P, C, L], F32R), sb("ht_lo", [P, C, L], F32R)
        qkv = sb("qkv", [P, T, 3 * D])
        q_t, k_t, v_t = sb("q_t", [P, H, 32]), sb("k_t", [P, H, 32]), sb("v_t", [P, HD, 32])
        q_bd = sb("q_bd", [P, T, H, 32])
        s_max, s_sub = sb("s_max", [P, 32]), sb("s_sub", [P, 32, H])
        s_exp, s_sum, s_rec = sb("s_exp", [P, 32, H]), sb("s_sum", [P, 32]), sb("s_rec", [P, 32])
        p_bd, p_t = sb("p_bd", [P, 32, T, H]), sb("p_t", [P, 32, 32])
        o_tok = sb("o_tok", [P, T, D])
        ot_hi, ot_lo = sb("ot_hi", [P, C, L], F32R), sb("ot_lo", [P, C, L], F32R)
        y2 = sb("y2", [P, T, D])
        ms, r2 = sb("ms", [P, T]), sb("r2", [P, T])
        h2n = sb("h2n", [P, T, D])
        h2_hi, h2_lo = sb("h2_hi", [P, C, L], F32R), sb("h2_lo", [P, C, L], F32R)
        gl = sb("gl", [E, L])
        ga, gb, gate = sb("ga", [P, T, E]), sb("gb", [P, T, E]), sb("gate", [P, T, E])
        gm, gr = sb("gm", [P, T]), sb("gr", [P, T])
        acc = [[sb(f"acc{t}_{n}", [P, D]) for n in range(2)] for t in range(T)]
        outb = [sb(f"outb{n}", [P, T, D]) for n in range(2)]

        stage_d = sb("stage_d", [P, C, R])
        stage_u = sb("stage_u", [R, 2 * D])
        stage_g = sb("stage_g", [P, C, P])
        stage_f = sb("stage_f", [P, 4, P])
        wdn_t = sb("wdn_t", [R, C, P])
        bdn_col, bdn_wide = sb("bdn_col", [R, 1]), sb("bdn_wide", [R, P])
        gamma1, gamma2 = sb("gamma1", [P, C]), sb("gamma2", [P, C])

        W = []

        def w(name, eng, waits, run, dma=False):
            W.append(Step(name, eng, 100, waits, run, dma))

        def const_tri(e, b):
            return e.affine_select(out=causal[:, :], in_=causal[:, :], compare_op=ALU.is_ge, fill=0.0,
                                   base=0, pattern=[[1, P]], channel_multiplier=-1)

        w("zero_id", "pool", [], lambda e, b: e.memset(ident[:, :], 0.0))
        w("one_tri", "pool", [], lambda e, b: e.memset(causal[:, :], 1.0))
        w("zero_f", "dve", [], lambda e, b: e.memset(stage_f[:, :, :], 0.0))
        w("zero_g", "dve", [], lambda e, b: e.memset(stage_g[:, :, :], 0.0))
        w("half", "dve", [], lambda e, b: e.memset(neg_half[:, :], -0.5))
        w("ident", "pool", ["W.zero_id"], lambda e, b: e.affine_select(
            out=ident[:, :], in_=ident[:, :], compare_op=ALU.not_equal, fill=1.0, base=0,
            pattern=[[-1, P]], channel_multiplier=1))
        w("tri", "pool", ["W.one_tri"], const_tri)

        w("h_sel", "dve", ["W.ident"], lambda e, b: e.tensor_tensor(
            h_sel[:, :, :].rearrange("p a (e m) -> p (a e) m", m=M),
            ident[0:R, 0:H].unsqueeze(2).to_broadcast([R, H, M]),
            ident[0:R, 32:32 + H].unsqueeze(2).to_broadcast([R, H, M]), ALU.add))

        loads = [
            ("ld_gx", lambda: (g_cols[:, 0:1], gx_d.rearrange("(a n) -> a n", a=1).to_broadcast([P, 1]))),
            ("ld_gf", lambda: (g_cols[:, 1:2], gf_d.rearrange("(a n) -> a n", a=1).to_broadcast([P, 1]))),
            ("ld_g1", lambda: (gamma1[:, :], g1_d.rearrange("(c p) -> p c", p=P))),
            ("ld_g2", lambda: (gamma2[:, :], g2_d.rearrange("(c p) -> p c", p=P))),
            ("ld_q", lambda: (stage_q[:, :, :], wq_d.rearrange("(c p) n -> p c n", p=P))),
            ("ld_dn", lambda: (stage_d[:, :, :], wdn_d.rearrange("(c p) n -> p c n", p=P))),
            ("ld_bdn", lambda: (bdn_col[:, :], bdn_d.rearrange("(p a) -> p a", a=1))),
            ("ld_up", lambda: (stage_u[:, :], wup_d)),
            ("ld_bq", lambda: (b_qkv[:, 0:D], bq_d.rearrange("(a n) -> a n", a=1).to_broadcast([P, D]))),
            ("ld_bup", lambda: (b_qkv[:, D:3 * D], bup_d.rearrange("(a n) -> a n", a=1).to_broadcast([P, 2 * D]))),
            ("ld_o", lambda: (stage_o[:, :, :], wo_d.rearrange("(c p) n -> p c n", p=P))),
            ("ld_bo", lambda: (b_o[:, :], bo_d.rearrange("(a n) -> a n", a=1).to_broadcast([P, D]))),
            ("ld_bg", lambda: (b_g[:, :], bg_d.rearrange("(a n) -> a n", a=1).to_broadcast([P, E]))),
        ]
        for name, ops in loads:
            w(name, "act", [], lambda e, b, ops=ops: e.dma_start(*ops()), dma=True)
        w("ld_g", "act", ["W.zero_g"], lambda e, b: e.dma_start(
            stage_g[:, :, 0:E], wg_d.rearrange("(c p) n -> p c n", p=P)), dma=True)
        for c in range(C):
            w(f"ld_e{c}", "act", [], lambda e, b, c=c: e.dma_start(
                stage[:, c * E * D:(c + 1) * E * D].rearrange("p (e f) -> p e f", e=E),
                we_d[:, c * P:(c + 1) * P, :].rearrange("e p f -> p e f")), dma=True)
        for h in range(8):
            w(f"ld_f{h}", "act", ["W.zero_f"], lambda e, b, h=h: e.dma_start(
                stage_f[HD * h:HD * h + HD, h // 2, M * (h % 2):M * (h % 2) + M], rf_d), dma=True)

        def split(name, hi, lo, src, waits):
            w(name + "_hi", "dve", waits, lambda e, b: e.tensor_copy(hi, src))
            w(name + "_lo", "dve", [f"W.{name}_hi"], lambda e, b: e.tensor_tensor(
                lo, src, hi.bitcast(F32), ALU.subtract))

        def sel_tok_run(e, b):
            v = ident[:, :].rearrange("p (a t k) -> p t a k", t=2, k=HD)
            return e.tensor_reduce(sel_tok[:, :], v, AX.XY, ALU.add)

        w("sel_tok", "dve", ["W.ident"], sel_tok_run)
        w("tanh", "act", ["W.ld_gx", "W.ld_gf"], lambda e, b: (
            e.activation(tanh_x[:, :], g_cols[:, 0:1], ACT.Tanh),
            e.activation(tanh_f[:, :], g_cols[:, 1:2], ACT.Tanh))[1])
        w("f_scale", "dve", [f"W.ld_f{h}" for h in range(8)], lambda e, b: e.tensor_scalar(
            stage_f[:, :, :], stage_f[:, :, :], QK_SCALE, None, ALU.mult))
        split("wf", wf_hi[:, :, :], wf_lo[:, :, :], stage_f[:, :, :], ["W.f_scale"])

        def by_gamma(tile, gamma):
            def run(e, b):
                for c in range(C):
                    last = e.tensor_scalar(tile(c), tile(c), gamma[:, c:c + 1], None, ALU.mult)
                return last
            return run

        w("q_gamma", "dve", ["W.ld_q", "W.ld_g1"], lambda e, b: [
            e.tensor_scalar(qkv32[:, c, 0:D], stage_q[:, c, :], gamma1[:, c:c + 1], None, ALU.mult)
            for c in range(C)][-1])
        w("d_gamma", "dve", ["W.ld_dn", "W.ld_g1"], by_gamma(lambda c: stage_d[:, c, :], gamma1))
        w("g_gamma", "dve", ["W.ld_g", "W.ld_g2"], by_gamma(lambda c: stage_g[:, c, :], gamma2))
        w("e_gamma", "dve", ["W.ld_e0", "W.ld_e1", "W.ld_g2"],
          by_gamma(lambda c: stage[:, c * E * D:(c + 1) * E * D], gamma2))
        w("bdn_wide", "dve", ["W.ld_bdn"], lambda e, b: e.tensor_copy(
            bdn_wide[:, :], bdn_col[:, 0:1].to_broadcast([R, P])))
        w("dn_t", "pe", ["W.d_gamma", "W.ident"], lambda e, b: [
            e.transpose(f_ps[0:R, c, 0:P], stage_d[:, c, :], ident[:, :]) for c in range(C)][-1])
        w("dn_t_sb", "dve", ["W.dn_t"], lambda e, b: e.tensor_copy(wdn_t[:, :, :], f_ps[0:R, 0:C, 0:P]))
        w("kv", "pe", ["W.dn_t_sb", "W.ld_up"], lambda e, b: [
            e.matmul(f_ps[:, c, :], wdn_t[:, c, :], stage_u[:, :], start=True, stop=True)
            for c in range(C)][-1])
        w("bkv", "pe", ["W.bdn_wide", "W.ld_up"], lambda e, b: e.matmul(
            f_ps[:, C, :], bdn_wide[:, :], stage_u[:, :], start=True, stop=True))

        def kv_sb(e, b):
            for c in range(C):
                for s in range(2):
                    last = e.tensor_copy(
                        qkv32[:, c, D * (1 + s):D * (2 + s)].rearrange("p (g d) -> p g d", d=HD),
                        f_ps[:, c, :].rearrange("p (g s d) -> p s g d", s=2, d=HD)[:, s])
            return last

        w("kv_sb", "dve", ["W.kv"], kv_sb)
        w("bkv_sum", "dve", ["W.bkv", "W.ld_bup"], lambda e, b: e.tensor_tensor(
            stage_o2[:, :], f_ps[:, C, :], b_qkv[:, D:3 * D], ALU.add))
        w("bkv_sb", "dve", ["W.bkv_sum"], lambda e, b: [
            e.tensor_copy(b_qkv[:, D * (1 + s):D * (2 + s)].rearrange("p (g d) -> p g d", d=HD),
                          stage_o2[:, :].rearrange("p (g s d) -> p s g d", s=2, d=HD)[:, s])
            for s in range(2)][-1])
        split("wqkv", wqkv_hi[:, :, :], wqkv_lo[:, :, :], qkv32[:, :, :], ["W.kv_sb", "W.q_gamma"])
        split("wo", wo_hi[:, :, :], wo_lo[:, :, :], stage_o[:, :, :], ["W.ld_o"])
        split("wg", wg_hi[:, :, :], wg_lo[:, :, :], stage_g[:, :, :], ["W.g_gamma"])
        split("we", we_hi[:, :, :].rearrange("p a b -> p (a b)"),
              we_lo[:, :, :].rearrange("p a b -> p (a b)"), stage[:, :], ["W.e_gamma"])

        A = []
        A.append(Step("load", "sp", 100, ["A.square--"], lambda e, b: e.dma_start(
            c_chunk[b.par][:, :, :],
            ctx_d[bass.ds(b.times(CH), CH), :, :].rearrange("b (t p) d -> p (b t) d", p=P)), dma=True))
        A.append(Step("square", "act", 1900, ["A.load"], lambda e, b: e.activation(
            c_chunk[b.par][:, :, :], c_chunk[b.par][:, :, :], ACT.Square, scale=QK_SCALE)))
        A.append(Step("sum", "dve", 2200, ["A.square"], lambda e, b: e.tensor_reduce(
            hk[:, bass.ds(b.times(CH * T), CH * T), :],
            c_chunk[b.par][:, :, :].rearrange("p n (h d) -> p n h d", d=HD), AX.X, ALU.add)))
        A[0].waits = ["A.sum--"]

        S = []
        last_chunk = NB // CH - 1

        def s(name, eng, waits, run):
            S.append(Step(name, eng, 100, waits, run))

        s("min", "dve", ["A.end"], lambda e, b: e.tensor_reduce(
            hk_min[:, :], hk[:, :, :], AX.XY, ALU.min))
        s("col", "dve", ["S.min"], lambda e, b: e.tensor_scalar(
            hk_col[:, :], hk_min[:, :], -0.5, None, ALU.mult))
        s("stab", "pool", ["S.col"], lambda e, b: e.partition_all_reduce(
            stab[:, :], hk_col[:, :], P, bass.bass_isa.ReduceOp.max))
        s("less", "dve", ["S.stab"], lambda e, b: e.tensor_scalar(
            hk[:, :, :], hk[:, :, :], -0.5, stab[:, 0:1], ALU.mult, ALU.subtract))

        x_in = [sb(f"x_in{p}", [P, T, D]) for p in range(2)]
        c_in = [sb(f"c_in{p}", [P, T, D]) for p in range(2)]
        x1 = [sb(f"x1_{p}", [P, T, D]) for p in range(2)]
        bn6, mv = sb("bn6", [P, T, 6]), sb("mv", [P, T, 2])
        var_e, rstd = sb("var_e", [P, T]), sb("rstd", [P, T])
        xn = sb("xn", [P, T, D])
        q_hi, q_lo = sb("q_hi", [P, C, L], F32R), sb("q_lo", [P, C, L], F32R)
        k_hi, k_lo = sb("k_hi", [P, C, L], F32R), sb("k_lo", [P, C, L], F32R)
        h2 = sb("h2", [P, T, R])
        h_t = sb("h_t", [R, L], F32R)
        v1 = sb("v1", [P, T, H, 32])
        qf, kf = sb("qf", [P, PAIRS, L]), sb("kf", [P, PAIRS, L])
        att = [sb(f"att{n}", [P, 4, 3 * P]) for n in range(2)]
        nt = sb("nt", [P, QUADS, L])
        den3 = sb("den3", [P, 3, T, H])
        o_x = sb("o_x", [P, T, D])

        Qn, Pn = [], []

        def q_(name, eng, ns, waits, run, dma=False, kind=""):
            Qn.append(Step(name, eng, ns, waits, run, dma, kind))

        def p(name, eng, ns, waits, run, dma=False, kind=""):
            Pn.append(Step(name, eng, ns, waits, run, dma, kind))

        def rows(dram, b):
            return dram[bass.ds(b.times(1), 1), :, :].rearrange("b (t p) d -> p (b t) d", p=P)

        q_("x_load", "sp", 2000, ["P.x1--"], lambda e, b: e.dma_start(x_in[b.par][:, :, :], rows(x_d, b)), True)
        q_("c_load", "sp", 2000, ["P.x1--"],
          lambda e, b: e.dma_start(c_in[b.par][:, :, :], rows(ctx_d, b)), True)

        q_("bn", "dve", 700, ["Q.x_load", "Q.bn_agg-"], lambda e, b: [
            e.bn_stats(bn6[:, t, :], x_in[b.par][:, t, :]) for t in range(T)][-1])
        q_("bn_agg", "dve", 150, ["Q.bn", "Q.xn-"], lambda e, b: [
            e.bn_aggr(mv[:, t, :], bn6[:, t, :]) for t in range(T)][-1], kind="aggr")
        q_("var_e", "dve", 70, ["Q.bn_agg", "Q.rstd-"], lambda e, b: e.tensor_scalar(
            var_e[:, :], mv[:, :, 1], LN_EPS, None, ALU.add))
        q_("rstd", "pool", 300, ["Q.var_e", "Q.xn-", "W.half"], lambda e, b: e.tensor_tensor(
            rstd[:, :], var_e[:, :], neg_half[:, 0:T], ALU.pow))
        q_("xn", "dve", 450, ["Q.rstd", "Q.x_t-"], lambda e, b: [
            e.tensor_scalar(xn[:, t, :], x_in[b.par][:, t, :], mv[:, t, 0:1], rstd[:, t:t + 1],
                            ALU.subtract, ALU.mult) for t in range(T)][-1])

        def turn(bank, src):
            def run(e, b):
                for c in range(C):
                    for t in range(T):
                        last = e.transpose(bank(c)[:, t * P:(t + 1) * P],
                                           src(b)[:, t, c * P:(c + 1) * P], ident[:, :])
                return last
            return run

        def h2_run(e, b):
            src = hk[:, bass.ds(b.times(T), T), :]
            return e.activation(h2[:, :, 0:H].bitcast(F32R), src, ACT.Copy)

        q_("h_hi", "act", 250, ["S.zero_h2", "P.h_tr-", "Q.h_lo-"], h2_run)
        q_("h_lo", "dve", 120, ["Q.h_hi"], lambda e, b: e.tensor_tensor(
            h2[:, :, 32:32 + H], hk[:, bass.ds(b.times(T), T), :], h2[:, :, 0:H], ALU.subtract))
        p("v1", "pool", 600, ["Q.c_load", "P.av3-", "S.one_v1"], lambda e, b: e.tensor_copy(
            v1[:, :, :, 0:HD], c_in[b.par][:, :, :].rearrange("p t (h d) -> p t h d", d=HD)), kind="scalar")
        q_("c_t", "pe", 500, ["Q.c_load", "P.o_x-", "W.ident"],
          turn(lambda c: n_ps[:, 1, c * L:(c + 1) * L], lambda b: c_in[b.par]))
        q_("k_hi", "act", 620, ["Q.c_t"], lambda e, b: e.activation(
            k_hi[:, :, :].rearrange("p a b -> p (a b)"), n_ps[:, 1, :], ACT.Copy))
        q_("k_lo", "dve", 620, ["Q.k_hi"], lambda e, b: e.tensor_tensor(
            k_lo[:, :, :].rearrange("p a b -> p (a b)"), n_ps[:, 1, :],
            k_hi[:, :, :].rearrange("p a b -> p (a b)").bitcast(F32), ALU.subtract))
        bank, free = P_BANKS["h_t"]
        p("h_tr", "pe", 250, ["Q.h_lo", free], lambda e, b, bank=bank: [
            e.transpose(p_ps[0:R, bank, t * P:(t + 1) * P], h2[:, t, :], ident[:, :]) for t in range(T)][-1], kind="small")
        p("h_t", "act", 420, ["P.h_tr"], lambda e, b, bank=bank: e.activation(
            h_t[:, :], p_ps[0:R, bank, 0:L], ACT.Copy))
        q_("x_t", "pe", 500, ["Q.xn", "Q.k_lo"],
          turn(lambda c: n_ps[:, 1, c * L:(c + 1) * L], lambda b: xn))
        q_("q_hi", "act", 620, ["Q.x_t"], lambda e, b: e.activation(
            q_hi[:, :, :].rearrange("p a b -> p (a b)"), n_ps[:, 1, :], ACT.Copy))
        q_("q_lo", "dve", 620, ["Q.q_hi"], lambda e, b: e.tensor_tensor(
            q_lo[:, :, :].rearrange("p a b -> p (a b)"), n_ps[:, 1, :],
            q_hi[:, :, :].rearrange("p a b -> p (a b)").bitcast(F32), ALU.subtract))

        def features(src_hi, src_lo, n, bank, with_h):
            def run(e, b):
                for half in range(2):
                    pr = 2 * n + half
                    c, r = divmod(pr, 4)
                    ps = p_ps[:, bank, half * L:(half + 1) * L]
                    e.matmul(ps, wf_hi[:, r, :], src_hi[:, c, :], start=True, stop=False)
                    e.matmul(ps, wf_lo[:, r, :], src_hi[:, c, :], start=False, stop=False)
                    last = e.matmul(ps, wf_hi[:, r, :], src_lo[:, c, :], start=False, stop=not with_h)
                    if with_h:
                        last = e.matmul(ps, h_sel[:, pr, :], h_t[:, :], start=False, stop=True)
                return last
            return run

        for key, hi, lo, dst in (("k", k_hi, k_lo, kf), ("q", q_hi, q_lo, qf)):
            pass
        order = [("q", q_hi, q_lo, qf), ("k", k_hi, k_lo, kf)]
        for key, hi, lo, dst in order:
            for n in range(4):
                bank, free = P_BANKS[f"{key}_exp{n}"]
                waits = [f"Q.{key}_lo", free] + (["P.h_t"] if key == "k" else [])
                p(f"{key}_mm{n}", "pe", 970 if key == "k" else 720, waits + ["W.wf_lo", "W.h_sel"],
                  features(hi, lo, n, bank, key == "k"))
                flat = dst[:, 2 * n:2 * n + 2, :].rearrange("p a b -> p (a b)")
                p(f"{key}_exp{n}", "act", 620, [f"P.{key}_mm{n}", "P.a_mm_diag13-"],
                  lambda e, b, bank=bank, flat=flat: e.activation(flat, p_ps[:, bank, :], ACT.Exp))
                p(f"{key}f{n}", "pool", 600, [f"P.{key}_exp{n}"],
                  lambda e, b, flat=flat: e.tensor_scalar(flat, flat, KERNEL_EPS, 1.0, ALU.add, ALU.mult), kind="scalar")

        def head(q, j):
            return 8 * (q // 2) + 2 * j + q % 2

        def scores(q, bank, tk, tq):
            def run(e, b):
                for j in range(4):
                    pr, half = divmod(head(q, j), 2)
                    rows_ = slice(M * half, M * half + M)
                    last = e.matmul(p_ps[:, bank, j * P:(j + 1) * P],
                                    kf[rows_, pr, tk * P:(tk + 1) * P],
                                    qf[rows_, pr, tq * P:(tq + 1) * P], start=True, stop=True)
                return last
            return run

        def av(q):
            def run(e, b):
                bank, col = divmod(q * L, 512)
                for part in range(2):
                    for j in range(4):
                        h = head(q, j)
                        out = n_ps[32 * j:32 * j + 32, bank, col + part * P:col + L]
                        a = att[q % 2][:, j, 2 * part * P:2 * P + part * P]
                        last = e.matmul(out, v1[:, part, h, :], a, start=(part == 0), stop=(part == 1),
                                        skip_group_check=True, tile_position=(0, 32 * j))
                return last
            return run

        for q in range(QUADS):
            banks = []
            for kind, tk, tq in (("diag0", 0, 0), ("cross", 0, 1), ("diag1", 1, 1)):
                bank, free = P_BANKS[f"a_{kind}{q}"]
                banks.append(bank)
                p(f"a_mm_{kind}{q}", "pe", 900, [free, f"P.qf{q | 1}", f"P.kf{q | 1}"], scores(q, bank, tk, tq))
            reader = f"P.av{q - 2}" if q >= 2 else f"P.av{q + 2}-"
            mask = causal[:, :].unsqueeze(1).to_broadcast([P, 4, P])

            def masked(q, bank, col):
                return lambda e, b: e.tensor_tensor(
                    att[q % 2][:, :, col:col + P],
                    p_ps[:, bank, :].rearrange("p (j l) -> p j l", j=4), mask, ALU.mult)

            p(f"a_diag0{q}", "dve", 620, [f"P.a_mm_diag0{q}", reader, "W.tri"], masked(q, banks[0], 0))
            p(f"a_cross{q}", "act", 620, [f"P.a_mm_cross{q}", reader], lambda e, b, q=q, bank=banks[1]: e.activation(
                att[q % 2][:, :, P:2 * P], p_ps[:, bank, :].rearrange("p (j l) -> p j l", j=4), ACT.Copy))
            p(f"a_diag1{q}", "dve", 620, [f"P.a_mm_diag1{q}", reader], masked(q, banks[2], 2 * P))
            if q:
                p(f"av{q - 1}", "pe", 650, [f"P.a_diag1{q - 1}", f"P.a_cross{q - 1}", "P.v1", "Q.q_lo", "G.ht_lo-"],
                  av(q - 1))
        p(f"av{QUADS - 1}", "pe", 650, [f"P.a_diag1{QUADS - 1}", f"P.a_cross{QUADS - 1}"], av(QUADS - 1))

        p("nt", "act", 1050, [f"P.av{QUADS - 1}", "P.nt_t-"], lambda e, b: e.activation(
            nt[:, :, :].rearrange("p a b -> p (a b)"), n_ps[:, :, :].rearrange("p a b -> p (a b)"), ACT.Copy))
        p("nt_t", "pe", 1000, ["P.nt"], lambda e, b: [
            e.transpose(n_ps[:, t, :].rearrange("p (a j s v) -> p a s j v", a=2, s=2, v=32)[:, q // 2, q % 2],
                        nt[:, q, t * P:(t + 1) * P], ident[:, :])
            for t in range(T) for q in range(QUADS)][-1])
        nd = n_ps[:, :, :].rearrange("p t (h v) -> p t h v", v=32)
        p("den_small", "dve", 100, ["P.nt_t", "P.den-"], lambda e, b: e.tensor_scalar(
            den3[:, 0], nd[:, :, :, HD], M * NORM_STAB, None, ALU.is_le))
        p("den", "dve", 100, ["P.den_small"], lambda e, b: e.scalar_tensor_tensor(
            out=den3[:, 1], in0=den3[:, 0], scalar=2.0 * M * NORM_STAB, in1=nd[:, :, :, HD],
            op0=ALU.mult, op1=ALU.add))
        p("recip", "dve", 100, ["P.den"], lambda e, b: e.reciprocal(den3[:, 2], den3[:, 1]))
        p("recip_g", "dve", 70, ["P.recip", "W.tanh"], lambda e, b: e.tensor_scalar(
            den3[:, 1], den3[:, 2], tanh_x[:, 0:1], None, ALU.mult))
        p("o_x", "dve", 620, ["P.recip_g"], lambda e, b: [e.tensor_tensor(
            o_x[:, t, :].rearrange("p (h d) -> p h d", d=HD), nd[:, t, :, 0:HD],
            den3[:, 1, t, :].unsqueeze(2).to_broadcast([P, H, HD]), ALU.mult) for t in range(T)][-1])
        p("x1", "dve", 620, ["P.o_x", "Q.x_load", "F.out--"], lambda e, b: e.tensor_tensor(
            x1[b.par][:, :, :], o_x[:, :, :], x_in[b.par][:, :, :], ALU.add))

        s("zero_h2", "dve", [], lambda e, b: e.memset(h2[:, :, :], 0.0))
        s("zero_v1", "dve", [], lambda e, b: e.memset(v1[:, :, :, :], 0.0))
        s("one_v1", "dve", ["S.zero_v1"], lambda e, b: e.memset(v1[:, :, :, HD:HD + 1], 1.0))

        Fn = []
        def f(name, eng, ns, waits, run, dma=False, kind=""):
            Fn.append(Step(name, eng, ns, waits, run, dma, kind))

        Gn = []

        def g(name, eng, ns, waits, run, dma=False, kind=""):
            Gn.append(Step(name, eng, ns, waits, run, dma, kind))

        g("bn", "dve", 700, ["P.x1", "G.bn_agg-"], lambda e, b: [
            e.bn_stats(bn6g[:, t, :], x1[b.par][:, t, :]) for t in range(T)][-1])
        g("bn_agg", "dve", 150, ["G.bn", "G.hn-"], lambda e, b: [
            e.bn_aggr(mvg[:, t, :], bn6g[:, t, :]) for t in range(T)][-1], kind="aggr")
        g("var", "dve", 140, ["G.bn_agg", "G.rstd-"], lambda e, b: (
            e.tensor_scalar(var_f[:, 0, :], mvg[:, :, 1], LN_EPS, None, ALU.add),
            e.tensor_scalar(var_f[:, 1, :], mvg[:, :, 1], 1.0 + RMS_EPS, RMS_EPS * LN_EPS,
                            ALU.mult, ALU.add))[1])
        g("rstd", "pool", 300, ["G.var", "G.hn-"], lambda e, b: e.tensor_tensor(
            r_f[:, :, :].rearrange("p a b -> p (a b)"), var_f[:, :, :].rearrange("p a b -> p (a b)"),
            neg_half[:, 0:2 * T], ALU.pow))
        def norm(dst, which):
            return lambda e, b: [e.tensor_scalar(
                dst[:, t, :], x1[b.par][:, t, :], mvg[:, t, 0:1], r_f[:, which, t:t + 1],
                ALU.subtract, ALU.mult) for t in range(T)][-1]
        g("hn", "dve", 450, ["G.rstd", "G.h_t-"], norm(hn, 1))
        g("y", "dve", 450, ["G.rstd", "G.yb-"], norm(y, 0))
        A_bo = b_o[:, :].unsqueeze(1).to_broadcast([P, T, D])
        g("yb", "pool", 1200, ["G.y", "F.y2-", "W.ld_bo"], lambda e, b: e.tensor_tensor(
            yb[:, :, :], y[:, :, :], A_bo, ALU.add))

        g("h_t", "pe", 500, ["G.hn", "P.o_x"], turn(lambda c: n_ps[:, 0, c * L:(c + 1) * L], lambda b: hn))
        g("ht_hi", "act", 620, ["G.h_t", "F.v_mm-"], lambda e, b: e.activation(
            ht_hi[:, :, :].rearrange("p a b -> p (a b)"), n_ps[:, 0, :], ACT.Copy))
        g("ht_lo", "dve", 620, ["G.ht_hi", "F.v_mm-"], lambda e, b: e.tensor_tensor(
            ht_lo[:, :, :].rearrange("p a b -> p (a b)"), n_ps[:, 0, :],
            ht_hi[:, :, :].rearrange("p a b -> p (a b)").bitcast(F32), ALU.subtract))

        def turn_c(name, src, waits, hi, lo, readers):
            for c in range(C):
                bank, free = F_BANKS[f"{readers}{c}"]
                f(f"{name}{c}", "pe", 250, waits + [free], lambda e, b, c=c, bank=bank: [
                    e.transpose(f_ps[:, bank, t * P:(t + 1) * P], src[:, t, c * P:(c + 1) * P],
                                ident[:, :]) for t in range(T)][-1])
                f(f"{name}_hi{c}", "act", 400, [f"F.{name}{c}"], lambda e, b, c=c, bank=bank:
                  e.activation(hi[:, c, :], f_ps[:, bank, 0:L], ACT.Copy))
                f(f"{readers}{c}", "dve", 380, [f"F.{name}_hi{c}"], lambda e, b, c=c, bank=bank:
                  e.tensor_tensor(lo[:, c, :], f_ps[:, bank, 0:L], hi[:, c, :].bitcast(F32), ALU.subtract))

        def three_passes(e, out, a_hi, a_lo, b_hi, b_lo):
            for c in range(C):
                e.matmul(out, a_hi(c), b_hi(c), start=(c == 0), stop=False)
                e.matmul(out, a_hi(c), b_lo(c), start=False, stop=False)
                last = e.matmul(out, a_lo(c), b_hi(c), start=False, stop=(c == C - 1))
            return last

        def tok(tile, t):
            return lambda c: tile[:, c, t * P:(t + 1) * P]

        def cols(tile, a, b_):
            return lambda c: tile[:, c, a:b_]

        for t in range(T):
            bank, free = F_BANKS[f"qk{t}"]
            f(f"qk_mm{t}", "pe", 1370, ["G.ht_lo", free, "W.wqkv_lo"], lambda e, b, t=t, bank=bank: three_passes(
                e, f_ps[:, bank, :], tok(ht_hi, t), tok(ht_lo, t),
                cols(wqkv_hi, 0, 2 * D), cols(wqkv_lo, 0, 2 * D)))
            f(f"qk{t}", "dve", 620, [f"F.qk_mm{t}", "F.k_t-", "W.bkv_sb", "W.ld_bq"], lambda e, b, t=t, bank=bank:
              e.tensor_tensor(qkv[:, t, 0:2 * D], f_ps[:, bank, :], b_qkv[:, 0:2 * D], ALU.add))
        bank, free = F_BANKS["vv"]

        def v_mm(e, b, bank=bank):
            for t in range(T):
                last = three_passes(e, f_ps[:, bank, t * D:(t + 1) * D], tok(ht_hi, t), tok(ht_lo, t),
                                    cols(wqkv_hi, 2 * D, 3 * D), cols(wqkv_lo, 2 * D, 3 * D))
            return last

        f("v_mm", "pe", 1440, [free], v_mm)
        f("vv", "dve", 620, ["F.v_mm", "F.v_t-"], lambda e, b, bank=bank: e.tensor_tensor(
            qkv[:, :, 2 * D:3 * D], f_ps[:, bank, :].rearrange("p (t n) -> p t n", t=T),
            b_qkv[:, 2 * D:3 * D].unsqueeze(1).to_broadcast([P, T, D]), ALU.add))

        def in_parts(name, ns, waits, run, bank):
            for part in range(PARTS):
                f(name if part == PARTS - 1 else f"{name}{part}", "pe", ns, [] if part else waits,
                  lambda e, b, part=part: run(e, bank, part), kind="small")

        def heads_of(a):
            return qkv[:, :, a:a + D].rearrange("p t (h d) -> p h t d", d=HD)

        f("q_t", "dve", 620, ["F.qk1", "F.q_bd-"], lambda e, b: e.transpose(q_t[:, :, :], heads_of(0)))
        f("q_bd", "dve", 650, ["F.q_t", "F.s_mm-", "W.sel_tok"], lambda e, b: [e.tensor_scalar(
            q_bd[:, t, :, :], q_t[:, :, :], sel_tok[:, t:t + 1], None, ALU.mult) for t in range(T)][-1])
        f("k_t", "dve", 620, ["F.qk1", "F.s_mm-"], lambda e, b: e.transpose(k_t[:, :, :], heads_of(D)))

        bank, free = F_BANKS["s_sub"]

        def s_mm(e, bank, part):
            for n in range(32 * part // PARTS, 32 * (part + 1) // PARTS):
                for j in range(4):
                    r = slice(32 * j, 32 * j + 32)
                    last = e.matmul(f_ps[r, bank, n * H:(n + 1) * H], q_bd[r, :, :, n], k_t[r, :, n],
                                    start=True, stop=True, tile_position=(32 * j, 32 * j))
            return last

        in_parts("s_mm", 1450, ["F.q_bd", "F.k_t", free], s_mm, bank)
        f("v_t", "dve", 620, ["F.vv", "F.pv-"], lambda e, b: e.transpose(
            v_t[:, :, :], qkv[:, :, 2 * D:3 * D].rearrange("p t (g d) -> p d t g", d=HD)))
        sc = f_ps[:, bank, :].rearrange("p (n g) -> p n g", g=H)

        def per_row(tile):
            return tile[:, :].unsqueeze(2).to_broadcast([P, 32, H])

        f("s_max", "dve", 620, ["F.s_mm", "F.s_sub-"], lambda e, b: e.tensor_reduce(
            s_max[:, :], sc, AX.X, ALU.max))
        f("s_sub", "dve", 620, ["F.s_max", "F.s_exp-"], lambda e, b: e.tensor_tensor(
            s_sub[:, :, :], sc, per_row(s_max), ALU.subtract))
        f("s_exp", "act", 620, ["F.s_sub", "F.s_norm-"], lambda e, b: e.activation(
            s_exp[:, :, :], s_sub[:, :, :], ACT.Exp, scale=float(HD) ** -0.5))
        f("s_sum", "dve", 620, ["F.s_exp"], lambda e, b: e.tensor_reduce(
            s_sum[:, :], s_exp[:, :, :], AX.X, ALU.add))
        f("s_rec", "dve", 90, ["F.s_sum"], lambda e, b: e.reciprocal(s_rec[:, :], s_sum[:, :]))
        f("s_norm", "dve", 620, ["F.s_rec"], lambda e, b: e.tensor_tensor(
            s_exp[:, :, :], s_exp[:, :, :], per_row(s_rec), ALU.mult))
        f("p_bd", "dve", 650, ["F.s_norm"], lambda e, b: [e.tensor_scalar(
            p_bd[:, :, t, :], s_exp[:, :, :], sel_tok[:, t:t + 1], None, ALU.mult) for t in range(T)][-1])
        f("p_t", "dve", 1150, ["F.p_bd", "F.pv-"], lambda e, b: e.transpose(
            p_t[:, :, :], p_bd[:, :, :, :].rearrange("p n t g -> p n (t g)")))
        bank, free = F_BANKS["o_tok"]

        def pv(e, bank, part):
            for n in range(32 * part // PARTS, 32 * (part + 1) // PARTS):
                for j in range(4):
                    r = slice(32 * j, 32 * j + 32)
                    last = e.matmul(f_ps[r, bank, n * HD:(n + 1) * HD], p_t[r, n, :], v_t[r, :, n],
                                    start=True, stop=True, tile_position=(32 * j, 32 * j))
            return last

        in_parts("pv", 1450, ["F.p_t", "F.v_t", free], pv, bank)
        f("o_tok", "dve", 620, ["F.pv", "F.o_tr-"], lambda e, b, bank=bank: e.transpose(
            o_tok[:, :, :].rearrange("p t (h d) -> p d t h", d=HD),
            f_ps[:, bank, :].rearrange("p (n d) -> p d n", d=HD)))

        bank, free = F_BANKS["ot_lo"]
        f("o_tr", "pe", 500, ["F.o_tok", free], lambda e, b, bank=bank: [
            e.transpose(f_ps[:, bank, c * L + t * P:c * L + (t + 1) * P], o_tok[:, t, c * P:(c + 1) * P],
                        ident[:, :]) for c in range(C) for t in range(T)][-1])
        f("ot_hi", "act", 620, ["F.o_tr"], lambda e, b, bank=bank: e.activation(
            ot_hi[:, :, :].rearrange("p a b -> p (a b)"), f_ps[:, bank, :], ACT.Copy))
        f("ot_lo", "dve", 620, ["F.ot_hi"], lambda e, b, bank=bank: e.tensor_tensor(
            ot_lo[:, :, :].rearrange("p a b -> p (a b)"), f_ps[:, bank, :],
            ot_hi[:, :, :].rearrange("p a b -> p (a b)").bitcast(F32), ALU.subtract))
        bank, free = F_BANKS["y2"]

        def o_mm(e, b, bank=bank):
            for t in range(T):
                last = three_passes(e, f_ps[:, bank, t * D:(t + 1) * D], tok(ot_hi, t), tok(ot_lo, t),
                                    cols(wo_hi, 0, D), cols(wo_lo, 0, D))
            return last

        f("o_mm", "pe", 1440, ["F.ot_lo", free, "W.wo_lo"], o_mm)
        f("y2", "dve", 620, ["F.o_mm", "G.yb", "F.e0_0a-", "F.e1_0a-", "F.h2n-"], lambda e, b, bank=bank:
          e.tensor_tensor(y2[:, :, :], f_ps[:, bank, :].rearrange("p (t n) -> p t n", t=T),
                          yb[:, :, :], ALU.add))
        f("bn2", "dve", 700, ["F.y2", "F.bn2_agg-"], lambda e, b: [
            e.bn_stats(bn6f[:, t, :], y2[:, t, :]) for t in range(T)][-1])
        f("bn2_agg", "dve", 150, ["F.bn2"], lambda e, b: [
            e.bn_aggr(mvf[:, t, :], bn6f[:, t, :]) for t in range(T)][-1], kind="aggr")
        f("ms0", "dve", 70, ["F.bn2_agg", "F.ms-"], lambda e, b: e.tensor_tensor(
            ms[:, :], mvf[:, :, 0], mvf[:, :, 0], ALU.mult))
        f("ms1", "dve", 70, ["F.ms0", "F.r2-"], lambda e, b: e.tensor_tensor(
            gm[:, :], ms[:, :], mvf[:, :, 1], ALU.add))
        f("ms", "dve", 70, ["F.ms1"], lambda e, b: e.tensor_scalar(
            ms[:, :], gm[:, :], RMS_EPS, None, ALU.add))
        f("r2", "pool", 300, ["F.ms", "F.h2n-"], lambda e, b: e.tensor_tensor(
            r2[:, :], ms[:, :], neg_half[:, 0:T], ALU.pow))
        f("h2n", "dve", 450, ["F.r2", "F.h2_t1-"], lambda e, b: [e.tensor_scalar(
            h2n[:, t, :], y2[:, t, :], r2[:, t:t + 1], None, ALU.mult) for t in range(T)][-1])
        turn_c("h2_t", h2n, ["F.h2n"], h2_hi, h2_lo, "h2_lo")

        bank, free = F_BANKS["ga"]
        f("g_mm", "pe", 730, ["F.h2_lo1", free, "W.wg_lo"], lambda e, b, bank=bank: three_passes(
            e, f_ps[:, bank, 0:L], lambda c: wg_hi[:, c, :], lambda c: wg_lo[:, c, :],
            lambda c: h2_hi[:, c, :], lambda c: h2_lo[:, c, :]))
        f("gl", "act", 420, ["F.g_mm", "F.g_t-"], lambda e, b, bank=bank: e.activation(
            gl[:, :], f_ps[0:E, bank, 0:L], ACT.Copy))
        
        f("g_t", "pe", 150, ["F.gl"], lambda e, b, bank=bank: [
            e.transpose(f_ps[:, bank, L + t * E:L + (t + 1) * E], gl[:, t * P:(t + 1) * P], ident[0:E, 0:E])
            for t in range(T)][-1], kind="small")
        f("ga", "dve", 90, ["F.g_t", "F.gb-", "W.ld_bg"], lambda e, b, bank=bank: e.tensor_tensor(
            ga[:, :, :], f_ps[:, bank, L:L + T * E].rearrange("p (t e) -> p t e", t=T),
            b_g[:, :].unsqueeze(1).to_broadcast([P, T, E]), ALU.add))
        f("gmax", "dve", 90, ["F.ga", "F.ms"], lambda e, b: e.tensor_reduce(gm[:, :], ga[:, :, :], AX.X, ALU.max))
        f("gb", "dve", 90, ["F.gmax", "F.gexp-"], lambda e, b: e.tensor_tensor(
            gb[:, :, :], ga[:, :, :], gm[:, :].unsqueeze(2).to_broadcast([P, T, E]), ALU.subtract))
        f("gexp", "act", 250, ["F.gb", "F.e1_3b-"], lambda e, b: e.activation(
            gate[:, :, :], gb[:, :, :], ACT.Exp))
        f("gsum", "dve", 90, ["F.gexp"], lambda e, b: e.tensor_reduce(gm[:, :], gate[:, :, :], AX.X, ALU.add))
        f("grec", "dve", 90, ["F.gsum"], lambda e, b: e.reciprocal(gr[:, :], gm[:, :]))
        f("gate", "dve", 90, ["F.grec"], lambda e, b: e.tensor_tensor(
            gate[:, :, :], gate[:, :, :], gr[:, :].unsqueeze(2).to_broadcast([P, T, E]), ALU.mult))

        for t in range(T):
            for n in range(4):
                bank, free = F_BANKS[f"e{t}_{n}b"]
                f(f"e_mm{t}_{n}", "pe", 1370, ["F.h2_lo1", free, "W.we_lo"], lambda e, b, t=t, n=n, bank=bank:
                  three_passes(e, f_ps[:, bank, :], tok(h2_hi, t), tok(h2_lo, t),
                               cols(we_hi, 2 * n * D, 2 * (n + 1) * D), cols(we_lo, 2 * n * D, 2 * (n + 1) * D)))
                for half in range(2):
                    ex = 2 * n + half
                    src = y2[:, t, :] if ex == 0 else acc[t][(ex - 1) % 2][:, :]
                    before = "F.gate" if ex == 0 else f"F.e{t}_{(ex - 1) // 2}{'ab'[(ex - 1) % 2]}"
                    waits = [f"F.e_mm{t}_{n}", before] + (["F.out-"] if ex == 1 else [])
                    f(f"e{t}_{n}{'ab'[half]}", "dve", 350, waits, lambda e, b, t=t, ex=ex, half=half, bank=bank, src=src:
                      e.scalar_tensor_tensor(out=acc[t][ex % 2][:, :], in0=f_ps[:, bank, half * D:(half + 1) * D],
                                             scalar=gate[:, t, ex:ex + 1], in1=src, op0=ALU.mult, op1=ALU.add))
        f("out", "dve", 700, ["F.e0_3b", "F.e1_3b", "F.store--", "W.tanh"], lambda e, b: [
            e.scalar_tensor_tensor(out=outb[b.par][:, t, :], in0=acc[t][1][:, :], scalar=tanh_f[:, 0:1],
                                   in1=x1[b.par][:, t, :], op0=ALU.mult, op1=ALU.add) for t in range(T)][-1])
        f("store", "sp", 50, ["F.out"], lambda e, b: e.dma_start(
            out_d[bass.ds(b.times(1), 1), :, :].rearrange("b (t p) d -> p (b t) d", p=P),
            outb[b.par][:, :, :]), True)

        for key, steps in (("W", W), ("A", A), ("S", S), ("Q", Qn), ("P", Pn), ("G", Gn), ("F", Fn)):
            streams[key] = Stream(key, steps, sem)

        names = {"pe": "tensor", "act": "scalar", "dve": "vector", "pool": "gpsimd", "sp": "sync"}
        body_order = merged([("Q", 1, Qn), ("P", 0, Pn), ("G", 0, Gn), ("F", -1, Fn)])
        ahead = {"Q": 1, "P": 0, "G": 0, "F": -1}

        def emit(eng_key, eng, key, steps, batch):
            for st in steps:
                if st.eng == eng_key:
                    streams[key].emit(st, eng, batch, streams)

        def first(st):
            return st.dma or st.eng == "pool" or st.name.startswith("zero")

        def program(eng_key, eng):
            emit(eng_key, eng, "W", [st for st in W if first(st)], Batch(0, 0))
            for k in range(2):
                emit(eng_key, eng, "A", A, Batch(0, k))
            if eng_key in ("sp", "act", "dve"):
                with eng.Fori(1, NB // CH // 2) as i:
                    for k in range(2):
                        emit(eng_key, eng, "A", A, Batch(i, k))
            emit(eng_key, eng, "W", [st for st in W if not first(st)], Batch(0, 0))
            emit(eng_key, eng, "S", S, Batch(0, 0))

            def body(i, k, keys="QPGF"):
                for key, st in body_order:
                    if st.eng == eng_key and key in keys:
                        streams[key].emit(st, eng, Batch(i, k + ahead[key]), streams)

            body(0, -1, "Q")
            body(0, 0, "QPG")
            body(0, 1)
            body(0, 2)
            with eng.Fori(0, (NB - 4) // 2) as i:
                body(i, 3)
                body(i, 4)
            last_i = (NB - 4) // 2
            body(last_i, 3, "PGF")
            body(last_i, 4, "F")
            if eng_key == "sp":
                for par in range(2):
                    st_sem, per_i, value = streams["F"].target("store", Batch(0, par))
                    eng.wait_ge(st_sem, (NB - 2) // 2 * per_i + value)

        streams["A"].place["end"] = streams["A"].place["sum"]
        end_steps = Step("end", "dve", 0, [], None)
        streams["A"].by_name["end"] = end_steps
        plain = streams["A"].target

        def a_target(name, batch):
            if name != "end":
                return plain(name, batch)
            sem_, _, value = plain("sum", Batch(0, last_chunk))
            return sem_, 0, value

        streams["A"].target = a_target

        block = ctx.enter_context(nc.Block())

        @block.sync
        def _(eng):
            program("sp", eng)

        @block.gpsimd
        def _(eng):
            program("pool", eng)

        @block.scalar
        def _(eng):
            program("act", eng)

        @block.vector
        def _(eng):
            program("dve", eng)

        @block.tensor
        def _(eng):
            program("pe", eng)


_INS = ['x', 'ctx_1024', 'g_xattn', 'g_ffn', 'L0_xattn_random_features', 'L0_ffn_gamma1', 'L0_ffn_Wq',
        'L0_ffn_bq', 'L0_ffn_Wdown', 'L0_ffn_bdown', 'L0_ffn_Wup', 'L0_ffn_bup', 'L0_ffn_Wo', 'L0_ffn_bo',
        'L0_ffn_gamma2', 'L0_ffn_Wg', 'L0_ffn_bg', 'L0_ffn_We']


def kernel(**inputs):
    import numpy as _np
    import concourse.bacc as _bacc
    from concourse import mybir as _mybir
    from concourse.bass_utils import run_bass_kernel_spmd as _run

    nc = _bacc.Bacc("TRN2", target_bir_lowering=False, num_devices=1)
    arrays, args = {}, []
    for name in _INS:
        a = _np.ascontiguousarray(inputs[name])
        arrays[f"in_{name}"] = a
        args.append(nc.dram_tensor(f"in_{name}", a.shape, _mybir.dt.from_np(a.dtype), kind="ExternalInput").ap())
    args.append(nc.dram_tensor("out_0", (NB, L, D), F32, kind="ExternalOutput").ap())
    build(nc, *args)
    r = _run(nc, [arrays], core_ids=[0])
    return r.results[0]["out_0"]
```

```python
from contextlib import ExitStack

import concourse.bass as bass
from concourse import mybir

F32 = mybir.dt.float32
F32R = mybir.dt.float32r
ALU = mybir.AluOpType
ACT = mybir.ActivationFunctionType
AX = mybir.AxisListType

P = 128
NB, L, D = 32, 256, 256
T = L // P
C = D // P
H, HD = 16, 16
M = 64
PAIRS = H * M // P
QUADS = H // 4
PARTS = 4
E = 8
R = 64
KERNEL_EPS, NORM_STAB = 1e-4, 1e-6
LN_EPS, RMS_EPS = 1e-5, 1e-6
QK_SCALE = D ** -0.25
CH = 4


SEPARATE_WAIT = {("dve", "aggr"), ("pe", "small"), ("pool", "scalar"), ("sp", "")}


BATCHED = "AQRPGFE"
AHEAD = {"Q": 1, "R": 1, "P": 0, "G": 0, "F": -1, "E": -2}


BEFORE_Q = ("half", "wf_h", "f_scale", "f_hi", "wf")


class Step:

    def __init__(self, name, eng, ns, waits, run, dma=False, kind=""):
        self.name, self.eng, self.ns, self.waits, self.run, self.dma = name, eng, ns, waits, run, dma
        self.kind = kind


class Batch:

    def __init__(self, i, k):
        self.i, self.k, self.par = i, k, k % 2

    def times(self, c, add=0):
        return self.i * (2 * c) + (self.k * c + add)

    def before(self, n):
        return Batch(self.i, self.k - n)

    def is_outside(self, n):
        return isinstance(self.i, int) and not 0 <= 2 * self.i + self.k - n < NB


def named(wait):
    name = wait.rstrip("+-")
    return name, wait.count("-") - wait.count("+")


class Stream:

    def __init__(self, key, steps, new_sem):
        self.key, self.steps = key, steps
        self.per_batch, self.place, self.sems = {}, {}, {}
        for s in steps:
            if s.dma:
                self.sems[s.name] = [new_sem(f"{key}_{s.name}_{p}") for p in range(2)]
                continue
            self.per_batch[s.eng] = self.per_batch.get(s.eng, 0) + 1
            self.place[s.name] = self.per_batch[s.eng]
            if s.eng not in self.sems:
                self.sems[s.eng] = new_sem(f"{key}_{s.eng}")
        self.by_name = {s.name: s for s in steps}

    def target(self, name, batch):
        s = self.by_name[name]
        if s.dma:
            return self.sems[name][batch.par], 16 * s.dma, (batch.k // 2 + 1) * 16 * s.dma
        c = self.per_batch[s.eng]
        return self.sems[s.eng], 2 * c, batch.k * c + self.place[name]

    def emit(self, step, eng, batch, streams):
        needed = {}
        for w in step.waits:
            name, back = named(w)
            key, name = name.split(".")
            at = batch if key in BATCHED else Batch(0, 0)
            if at.is_outside(back):
                continue
            sem, per_i, value = streams[key].target(name, at.before(back))
            per_i = per_i if key in BATCHED else 0
            if sem.name not in needed or needed[sem.name][2] < value:
                needed[sem.name] = (sem, per_i, value)
        waited = False
        for sem, per_i, value in needed.values():
            if waited and step.eng == "sp":
                eng.nop(nofuse=True)
            eng.wait_ge(sem, batch.i * per_i + value if per_i else value)
            waited = waited or bool(per_i) and not isinstance(batch.i, int)
        if waited and (step.eng, step.kind) in SEPARATE_WAIT:
            eng.nop(nofuse=True)
        last = step.run(eng, batch)
        if step.dma:
            for transfer in last if step.dma > 1 else [last]:
                transfer.then_inc(self.sems[step.name][batch.par], 16)
        else:
            last.then_inc(self.sems[step.eng], 1)


ORDER = """
    P.a_mm_diag00 P.a_mm_cross0 Q.x_load Q.h_hi P.a_diag00 P.a_mm_diag10 E.g_mm E.gl Q.c_load
    F.h_t F.ht_hi F.ht_lo Q.c_t Q.k_hi Q.bn Q.bn_agg E.g_t P.a_mm_diag01 Q.var_e E.ga P.v1
    P.a_diag10 Q.rstd F.qk_mm0 F.qk0 Q.xn Q.h_lo Q.k_lo E.gmax E.gb F.qk_mm1 F.v_mm F.qk1
    P.a_cross0 P.a_mm_cross1 E.gexp Q.h_tr Q.x_t F.vv Q.ks F.q_t F.q_bd F.k_t E.gsum
    P.a_mm_diag11 E.e_mm0_0 P.a_cross1 E.grec F.s_mm0 E.gate E.e0_0a E.e0_0b Q.h_t Q.q_hi
    F.s_mm1 E.e_mm0_1 F.v_t Q.q_lo F.s_mm2 P.a_diag01 F.s_mm P.a_diag11 E.e0_1a E.e0_1b F.s_max
    F.s_sub F.s_exp E.e_mm0_2 E.e0_2a E.e0_2b P.av0 P.a_mm_diag02 F.s_sum P.a_mm_cross2
    P.a_diag02 P.a_mm_diag12 P.av1 F.s_rec F.s_norm P.a_mm_diag03 F.p_bd E.e_mm0_3 F.p_t F.pv0
    E.e0_3a F.pv1 E.e0_3b E.e_mm1_0 E.e1_0a P.a_diag12 E.e1_0b P.a_cross2 F.pv2 F.pv F.o_tok
    E.e_mm1_1 F.o_tr F.ot_hi P.a_mm_cross3 P.a_cross3 P.a_mm_diag13 P.nt0 E.e1_1a F.ot_lo P.av2
    P.a_diag03 E.e1_1b F.o_mm P.a_diag13 F.y2 F.bn2 P.av3 Q.ks_h E.e_mm1_2 Q.qs F.bn2_agg F.ms0
    P.nt1 P.nt_t R.q_mm0 R.q_exp0 E.e1_2a R.q_mm1 R.q_mm2 F.ms F.r2 E.e1_2b R.qf0 P.den_small
    E.e_mm1_3 P.den P.recip R.q_exp1 R.q_mm3 R.q_exp2 R.q_exp3 R.qf1 P.o_x F.h2n R.k_mm0 R.k_mm1
    R.k_exp0 R.k_exp1 R.k_mm2 R.k_exp2 R.qf2 R.qf3 R.kf0 R.kf1 F.h2_t0 R.kf2 E.e1_3a E.e1_3b
    E.out P.x1 F.h2_t_hi0 F.h2_t1 R.k_mm3 R.k_exp3 G.bn F.h2_t_hi1 G.bn_agg G.var F.h2_lo0
    F.h2_lo1 G.rstd G.hn R.kf3 G.y G.yb E.store
""".split()


def in_order(lists):
    by_name = {f"{key}.{s.name}": (key, s) for key, steps in lists for s in steps}
    assert sorted(by_name) == sorted(ORDER)
    order = [by_name[name] for name in ORDER]
    for key, steps in lists:
        for eng in ("pe", "act", "dve", "pool", "sp"):
            assert [s for k, s in order if k == key and s.eng == eng] == [s for s in steps if s.eng == eng]
    return order


P_BANKS = {
    "q_exp0": (0, "P.a_cross3-"), "q_exp1": (1, "P.a_diag13-"), "q_exp2": (2, "P.a_diag03-"),
    "q_exp3": (0, "R.q_exp0"), "k_exp0": (1, "R.q_exp1"), "k_exp1": (2, "R.q_exp2"),
    "k_exp2": (0, "R.q_exp3"), "k_exp3": (1, "R.k_exp0"), "a_diag00": (2, "R.k_exp1"),
    "a_cross0": (0, "R.k_exp2"), "a_diag10": (1, "R.k_exp3"), "a_diag01": (2, "P.a_diag00"),
    "a_cross1": (0, "P.a_cross0"), "a_diag11": (1, "P.a_diag10"), "a_diag02": (2, "P.a_diag01"),
    "a_cross2": (0, "P.a_cross1"), "a_diag12": (1, "P.a_diag11"), "a_diag03": (2, "P.a_diag02"),
    "a_cross3": (0, "P.a_cross2"), "a_diag13": (1, "P.a_diag12"),
}
F_BANKS = {
    "qk0": (0, "F.h2_lo1-"), "qk1": (1, "F.h2_lo0-"), "vv": (0, "F.qk0"),
    "s_sub": (1, "F.qk1"), "o_tok": (0, "F.vv"), "ot_lo": (1, "F.s_sub"),
    "y2": (0, "F.o_tok"), "h2_lo0": (1, "F.ot_lo"), "h2_lo1": (0, "F.y2"),
}


def build(nc, x_d, ctx_d, gx_d, gf_d, rf_d, g1_d, wq_d, bq_d, wdn_d, bdn_d, wup_d, bup_d,
          wo_d, bo_d, g2_d, wg_d, bg_d, we_d, out_d):
    ctx = ExitStack()
    with ctx:
        def sb(name, shape, dt=F32):
            return ctx.enter_context(nc.sbuf_tensor(name, shape, dt))

        def sem(name):
            return ctx.enter_context(nc.semaphore(name))

        ctx.enter_context(nc.allow_non_contiguous_dma(reason="a few small parameter vectors"))

        p_ps = ctx.enter_context(nc.psum_tensor("p_ps", [P, 3, 512], F32))
        n_ps = ctx.enter_context(nc.psum_tensor("n_ps", [P, 2, 512], F32))
        f_ps = ctx.enter_context(nc.psum_tensor("f_ps", [P, 2, 512], F32))
        e_ps = ctx.enter_context(nc.psum_tensor("e_ps", [P, 512], F32))

        ident = sb("ident", [P, P])
        causal = sb("causal", [P, P])
        sel_tok = sb("sel_tok", [P, 2])
        neg_half = sb("neg_half", [P, 4])
        wf = sb("wf", [P, PAIRS, P], F32R)
        wqkv_hi, wqkv_lo = sb("wqkv_hi", [P, C, 3 * D], F32R), sb("wqkv_lo", [P, C, 3 * D], F32R)
        wo_hi, wo_lo = sb("wo_hi", [P, C, D], F32R), sb("wo_lo", [P, C, D], F32R)
        wg_hi, wg_lo = sb("wg_hi", [P, C, P], F32R), sb("wg_lo", [P, C, P], F32R)
        we_hi, we_lo = sb("we_hi", [P, C, E * D], F32R), sb("we_lo", [P, C, E * D], F32R)
        b_qkv = sb("b_qkv", [P, 3 * D])
        b_o = sb("b_o", [P, D])
        b_g = sb("b_g", [P, E])
        tanh_x, tanh_f = sb("tanh_x", [P, 1]), sb("tanh_f", [P, 1])
        g_cols = sb("g_cols", [P, 2])
        hk = sb("hk", [P, NB * T, H])
        hk_min, hk_col, stab = sb("hk_min", [P, 1]), sb("hk_col", [P, 1]), sb("stab", [P, 1])

        streams = {}

        early = ExitStack()
        stage = early.enter_context(nc.sbuf_tensor("stage", [P, C * E * D], F32))
        c_chunk = [early.enter_context(nc.sbuf_tensor(f"c_chunk{p}", [P, CH * T, D], F32)) for p in range(2)]
        stage_q = early.enter_context(nc.sbuf_tensor("stage_q", [P, C, D], F32))
        stage_o = early.enter_context(nc.sbuf_tensor("stage_o", [P, C, D], F32))
        qkv32 = early.enter_context(nc.sbuf_tensor("qkv32", [P, C, 3 * D], F32))
        stage_o2 = early.enter_context(nc.sbuf_tensor("stage_o2", [P, 2 * D], F32))
        stage_u = early.enter_context(nc.sbuf_tensor("stage_u", [R, 2 * D], F32))
        stage_g = early.enter_context(nc.sbuf_tensor("stage_g", [P, C, P], F32))
        stage_f = early.enter_context(nc.sbuf_tensor("stage_f", [96, P], F32))
        early.close()
        bn6f, mvf = sb("bn6f", [P, T, 6]), sb("mvf", [P, T, 2])
        bn6g, mvg = sb("bn6g", [P, T, 6]), sb("mvg", [P, T, 2])
        var_f, r_f = sb("var_f", [P, 2, T]), sb("r_f", [P, 2, T])
        y, yb, hn = sb("y", [P, T, D]), sb("yb", [P, T, D]), sb("hn", [P, T, D])
        ht_hi, ht_lo = sb("ht_hi", [P, C, L], F32R), sb("ht_lo", [P, C, L], F32R)
        qkv = sb("qkv", [P, T, 3 * D])
        q_t, k_t, v_t = sb("q_t", [P, H, 32]), sb("k_t", [P, H, 32]), sb("v_t", [P, HD, 32])
        q_bd = sb("q_bd", [P, T, H, 32])
        s_max, s_sub = sb("s_max", [P, 32]), sb("s_sub", [P, 32, H])
        s_exp, s_sum, s_rec = sb("s_exp", [P, 32, H]), sb("s_sum", [P, 32]), sb("s_rec", [P, 32])
        p_bd, p_t = sb("p_bd", [P, 32, T, H]), sb("p_t", [P, 32, 32])
        o_tok = sb("o_tok", [P, T, D])
        ot_hi, ot_lo = sb("ot_hi", [P, C, L], F32R), sb("ot_lo", [P, C, L], F32R)
        y2 = sb("y2", [P, T, D])
        sq, ms, r2 = sb("sq", [P, T]), sb("ms", [P, T]), sb("r2", [P, T])
        h2n = sb("h2n", [P, T, D])
        h2_hi, h2_lo = sb("h2_hi", [P, C, L], F32R), sb("h2_lo", [P, C, L], F32R)
        gl = sb("gl", [E, L])
        ga, gb, gate = sb("ga", [P, T, E]), sb("gb", [P, T, E]), sb("gate", [P, T, E])
        gm, gr = sb("gm", [P, T]), sb("gr", [P, T])
        acc = [[sb(f"acc{t}_{n}", [P, D]) for n in range(2)] for t in range(T)]
        outb = sb("outb", [P, T, D])

        stage_d = sb("stage_d", [P, C, R])

        wdn_t = sb("wdn_t", [R, C, P])
        bdn_col, bdn_wide = sb("bdn_col", [R, 1]), sb("bdn_wide", [R, P])
        gamma1, gamma2 = sb("gamma1", [P, C]), sb("gamma2", [P, C])

        W = []

        def w(name, eng, waits, run, dma=False):
            W.append(Step(name, eng, 100, waits, run, dma))

        def const_tri(e, b):
            return e.affine_select(out=causal[:, :], in_=causal[:, :], compare_op=ALU.is_ge, fill=0.0,
                                   base=0, pattern=[[1, P]], channel_multiplier=-1)

        w("zero_id", "pool", [], lambda e, b: e.memset(ident[:, :], 0.0))
        w("one_tri", "pool", [], lambda e, b: e.memset(causal[:, :], 1.0))
        w("zero_f", "dve", [], lambda e, b: e.memset(stage_f[:, :], 0.0))
        w("zero_g", "dve", [], lambda e, b: e.memset(stage_g[:, :, :], 0.0))
        w("half", "dve", [], lambda e, b: e.memset(neg_half[:, :], -0.5))
        w("ident", "pool", ["W.zero_id"], lambda e, b: e.affine_select(
            out=ident[:, :], in_=ident[:, :], compare_op=ALU.not_equal, fill=1.0, base=0,
            pattern=[[-1, P]], channel_multiplier=1))
        w("tri", "pool", ["W.one_tri"], const_tri)

        w("wf_h", "dve", ["W.ident"], lambda e, b: e.tensor_tensor(
            wf[96:P, :, :].rearrange("p a (e m) -> p (a e) m", m=M),
            ident[96:P, 96:96 + H].unsqueeze(2).to_broadcast([32, H, M]),
            ident[96:P, 112:112 + H].unsqueeze(2).to_broadcast([32, H, M]), ALU.add))

        loads = [
            ("ld_gx", lambda: (g_cols[:, 0:1], gx_d.rearrange("(a n) -> a n", a=1).to_broadcast([P, 1]))),
            ("ld_gf", lambda: (g_cols[:, 1:2], gf_d.rearrange("(a n) -> a n", a=1).to_broadcast([P, 1]))),
            ("ld_g1", lambda: (gamma1[:, :], g1_d.rearrange("(c p) -> p c", p=P))),
            ("ld_g2", lambda: (gamma2[:, :], g2_d.rearrange("(c p) -> p c", p=P))),
            ("ld_q", lambda: (stage_q[:, :, :], wq_d.rearrange("(c p) n -> p c n", p=P))),
            ("ld_dn", lambda: (stage_d[:, :, :], wdn_d.rearrange("(c p) n -> p c n", p=P))),
            ("ld_bdn", lambda: (bdn_col[:, :], bdn_d.rearrange("(p a) -> p a", a=1))),
            ("ld_up", lambda: (stage_u[:, :], wup_d)),
            ("ld_bq", lambda: (b_qkv[:, 0:D], bq_d.rearrange("(a n) -> a n", a=1).to_broadcast([P, D]))),
            ("ld_bup", lambda: (b_qkv[:, D:3 * D], bup_d.rearrange("(a n) -> a n", a=1).to_broadcast([P, 2 * D]))),
            ("ld_o", lambda: (stage_o[:, :, :], wo_d.rearrange("(c p) n -> p c n", p=P))),
            ("ld_bo", lambda: (b_o[:, :], bo_d.rearrange("(a n) -> a n", a=1).to_broadcast([P, D]))),
            ("ld_bg", lambda: (b_g[:, :], bg_d.rearrange("(a n) -> a n", a=1).to_broadcast([P, E]))),
        ]
        for name, ops in loads:
            w(name, "act", [], lambda e, b, ops=ops: e.dma_start(*ops()), dma=True)
        w("ld_g", "act", ["W.zero_g"], lambda e, b: e.dma_start(
            stage_g[:, :, 0:E], wg_d.rearrange("(c p) n -> p c n", p=P)), dma=True)
        for c in range(C):
            w(f"ld_e{c}", "act", [], lambda e, b, c=c: e.dma_start(
                stage[:, c * E * D:(c + 1) * E * D].rearrange("p (e f) -> p e f", e=E),
                we_d[:, c * P:(c + 1) * P, :].rearrange("e p f -> p e f")), dma=True)
        for n in range(6):
            w(f"ld_f{n}", "act", ["W.zero_f"], lambda e, b, n=n: e.dma_start(
                stage_f[HD * n:HD * (n + 1), M * (n % 2):M * (n % 2 + 1)], rf_d), dma=True)

        def split(name, hi, lo, src, waits):
            w(name + "_hi", "dve", waits, lambda e, b: e.tensor_copy(hi, src))
            w(name + "_lo", "dve", [f"W.{name}_hi"], lambda e, b: e.tensor_tensor(
                lo, src, hi.bitcast(F32), ALU.subtract))

        def sel_tok_run(e, b):
            v = ident[:, :].rearrange("p (a t k) -> p t a k", t=2, k=HD)
            return e.tensor_reduce(sel_tok[:, :], v, AX.XY, ALU.add)

        w("sel_tok", "dve", ["W.ident"], sel_tok_run)
        w("tanh", "act", ["W.ld_gx", "W.ld_gf"], lambda e, b: (
            e.activation(tanh_x[:, :], g_cols[:, 0:1], ACT.Tanh),
            e.activation(tanh_f[:, :], g_cols[:, 1:2], ACT.Tanh))[1])
        w("f_scale", "dve", [f"W.ld_f{n}" for n in range(6)], lambda e, b: e.tensor_scalar(
            stage_f[:, :], stage_f[:, :], QK_SCALE, None, ALU.mult))

        def every_pair(tile, a, b_):
            return tile[a:b_, :].unsqueeze(1).to_broadcast([b_ - a, PAIRS, P])

        w("f_hi", "dve", ["W.f_scale"], lambda e, b: e.tensor_copy(wf[0:96, :, :], every_pair(stage_f, 0, 96)))
        w("wf", "dve", ["W.f_hi", "W.wf_h"], lambda e, b: e.tensor_tensor(
            wf[64:96, :, :], every_pair(stage_f, 64, 96), wf[64:96, :, :].bitcast(F32), ALU.subtract))

        def by_gamma(tile, gamma):
            def run(e, b):
                for c in range(C):
                    last = e.tensor_scalar(tile(c), tile(c), gamma[:, c:c + 1], None, ALU.mult)
                return last
            return run

        w("q_gamma", "dve", ["W.ld_q", "W.ld_g1"], lambda e, b: [
            e.tensor_scalar(qkv32[:, c, 0:D], stage_q[:, c, :], gamma1[:, c:c + 1], None, ALU.mult)
            for c in range(C)][-1])
        w("d_gamma", "dve", ["W.ld_dn", "W.ld_g1"], by_gamma(lambda c: stage_d[:, c, :], gamma1))
        w("g_gamma", "dve", ["W.ld_g", "W.ld_g2"], by_gamma(lambda c: stage_g[:, c, :], gamma2))
        w("e_gamma", "dve", ["W.ld_e0", "W.ld_e1", "W.ld_g2"],
          by_gamma(lambda c: stage[:, c * E * D:(c + 1) * E * D], gamma2))
        w("bdn_wide", "dve", ["W.ld_bdn"], lambda e, b: e.tensor_copy(
            bdn_wide[:, :], bdn_col[:, 0:1].to_broadcast([R, P])))
        w("dn_t", "pe", ["W.d_gamma", "W.ident"], lambda e, b: [
            e.transpose(f_ps[0:R, c, 0:P], stage_d[:, c, :], ident[:, :]) for c in range(C)][-1])
        w("dn_t_sb", "dve", ["W.dn_t"], lambda e, b: e.tensor_copy(wdn_t[:, :, :], f_ps[0:R, 0:C, 0:P]))
        w("kv", "pe", ["W.dn_t_sb", "W.ld_up"], lambda e, b: [
            e.matmul(f_ps[:, c, :], wdn_t[:, c, :], stage_u[:, :], start=True, stop=True)
            for c in range(C)][-1])
        w("bkv", "pe", ["W.bdn_wide", "W.ld_up"], lambda e, b: e.matmul(
            e_ps[:, :], bdn_wide[:, :], stage_u[:, :], start=True, stop=True))

        def kv_sb(e, b):
            for c in range(C):
                for s in range(2):
                    last = e.tensor_copy(
                        qkv32[:, c, D * (1 + s):D * (2 + s)].rearrange("p (g d) -> p g d", d=HD),
                        f_ps[:, c, :].rearrange("p (g s d) -> p s g d", s=2, d=HD)[:, s])
            return last

        w("kv_sb", "dve", ["W.kv"], kv_sb)
        w("bkv_sum", "dve", ["W.bkv", "W.ld_bup"], lambda e, b: e.tensor_tensor(
            stage_o2[:, :], e_ps[:, :], b_qkv[:, D:3 * D], ALU.add))
        w("bkv_sb", "dve", ["W.bkv_sum"], lambda e, b: [
            e.tensor_copy(b_qkv[:, D * (1 + s):D * (2 + s)].rearrange("p (g d) -> p g d", d=HD),
                          stage_o2[:, :].rearrange("p (g s d) -> p s g d", s=2, d=HD)[:, s])
            for s in range(2)][-1])
        split("wqkv", wqkv_hi[:, :, :], wqkv_lo[:, :, :], qkv32[:, :, :], ["W.kv_sb", "W.q_gamma"])
        split("wo", wo_hi[:, :, :], wo_lo[:, :, :], stage_o[:, :, :], ["W.ld_o"])
        split("wg", wg_hi[:, :, :], wg_lo[:, :, :], stage_g[:, :, :], ["W.g_gamma"])
        split("we", we_hi[:, :, :].rearrange("p a b -> p (a b)"),
              we_lo[:, :, :].rearrange("p a b -> p (a b)"), stage[:, :], ["W.e_gamma"])

        A = []
        A.append(Step("load", "sp", 100, ["A.square--"], lambda e, b: e.dma_start(
            c_chunk[b.par][:, :, :],
            ctx_d[bass.ds(b.times(CH), CH), :, :].rearrange("b (t p) d -> p (b t) d", p=P)), dma=True))
        A.append(Step("square", "act", 1900, ["A.load"], lambda e, b: e.activation(
            c_chunk[b.par][:, :, :], c_chunk[b.par][:, :, :], ACT.Square, scale=QK_SCALE)))
        A.append(Step("sum", "dve", 2200, ["A.square"], lambda e, b: e.tensor_reduce(
            hk[:, bass.ds(b.times(CH * T), CH * T), :],
            c_chunk[b.par][:, :, :].rearrange("p n (h d) -> p n h d", d=HD), AX.X, ALU.add)))
        A[0].waits = ["A.sum--"]

        S = []
        last_chunk = NB // CH - 1

        def s(name, eng, waits, run):
            S.append(Step(name, eng, 100, waits, run))

        s("min", "dve", ["A.end"], lambda e, b: e.tensor_reduce(
            hk_min[:, :], hk[:, :, :], AX.XY, ALU.min))
        s("col", "dve", ["S.min"], lambda e, b: e.tensor_scalar(
            hk_col[:, :], hk_min[:, :], -0.5, None, ALU.mult))
        s("stab", "pool", ["S.col"], lambda e, b: e.partition_all_reduce(
            stab[:, :], hk_col[:, :], P, bass.bass_isa.ReduceOp.max))
        s("less", "dve", ["S.stab"], lambda e, b: e.tensor_scalar(
            hk[:, :, :], hk[:, :, :], -0.5, stab[:, 0:1], ALU.mult, ALU.subtract))

        x_in = [sb(f"x_in{p}", [P, T, D]) for p in range(2)]
        c_in = [sb(f"c_in{p}", [P, T, D]) for p in range(2)]
        x1 = [sb(f"x1_{p}", [P, T, D]) for p in range(2)]
        bn6, mv = sb("bn6", [P, T, 6]), sb("mv", [P, T, 2])
        var_e, rstd = sb("var_e", [P, T]), sb("rstd", [P, T])
        xn = sb("xn", [P, T, D])
        q_hi, q_lo = sb("q_hi", [P, C, L], F32R), sb("q_lo", [P, C, L], F32R)
        k_hi, k_lo = sb("k_hi", [P, C, L], F32R), sb("k_lo", [P, C, L], F32R)
        h2 = sb("h2", [P, T, 2 * H])
        h_t = sb("h_t", [2 * H, L], F32R)
        qs, ks = sb("qs", [96, PAIRS, L], F32R), sb("ks", [P, PAIRS, L], F32R)
        v1 = sb("v1", [P, T, H, 32])
        qf, kf = sb("qf", [P, PAIRS, L]), sb("kf", [P, PAIRS, L])
        att = [sb(f"att{n}", [P, 4, 3 * P]) for n in range(2)]
        nt = sb("nt", [P, QUADS, L])
        den3 = sb("den3", [P, 3, T, H])
        o_x = sb("o_x", [P, T, D])

        Qn, Rn, Pn = [], [], []

        def q_(name, eng, ns, waits, run, dma=False, kind=""):
            Qn.append(Step(name, eng, ns, waits, run, dma, kind))

        def p(name, eng, ns, waits, run, dma=False, kind=""):
            Pn.append(Step(name, eng, ns, waits, run, dma, kind))

        def rows(dram, b):
            return dram[bass.ds(b.times(1), 1), :, :].rearrange("b (t p) d -> p (b t) d", p=P)

        q_("x_load", "sp", 2000, ["P.x1--"], lambda e, b: e.dma_start(x_in[b.par][:, :, :], rows(x_d, b)), True)
        q_("c_load", "sp", 2000, ["P.x1--"],
          lambda e, b: e.dma_start(c_in[b.par][:, :, :], rows(ctx_d, b)), True)

        q_("bn", "dve", 700, ["Q.x_load", "Q.bn_agg-"], lambda e, b: [
            e.bn_stats(bn6[:, t, :], x_in[b.par][:, t, :]) for t in range(T)][-1])
        q_("bn_agg", "dve", 150, ["Q.bn", "Q.xn-"], lambda e, b: [
            e.bn_aggr(mv[:, t, :], bn6[:, t, :]) for t in range(T)][-1], kind="aggr")
        q_("var_e", "dve", 70, ["Q.bn_agg", "Q.rstd-"], lambda e, b: e.tensor_scalar(
            var_e[:, :], mv[:, :, 1], LN_EPS, None, ALU.add))
        q_("rstd", "pool", 300, ["Q.var_e", "Q.xn-", "W.half"], lambda e, b: e.tensor_tensor(
            rstd[:, :], var_e[:, :], neg_half[:, 0:T], ALU.pow))
        q_("xn", "dve", 450, ["Q.rstd", "Q.x_t-"], lambda e, b: [
            e.tensor_scalar(xn[:, t, :], x_in[b.par][:, t, :], mv[:, t, 0:1], rstd[:, t:t + 1],
                            ALU.subtract, ALU.mult) for t in range(T)][-1])

        def turn(bank, src):
            def run(e, b):
                for c in range(C):
                    for t in range(T):
                        last = e.transpose(bank(c)[:, t * P:(t + 1) * P],
                                           src(b)[:, t, c * P:(c + 1) * P], ident[:, :])
                return last
            return run

        def h2_run(e, b):
            src = hk[:, bass.ds(b.times(T), T), :]
            return e.activation(h2[:, :, 0:H].bitcast(F32R), src, ACT.Copy)

        q_("h_hi", "act", 250, ["Q.h_tr-", "Q.h_lo-", "S.less"], h2_run)
        q_("h_lo", "dve", 120, ["Q.h_hi"], lambda e, b: e.tensor_tensor(
            h2[:, :, H:2 * H], hk[:, bass.ds(b.times(T), T), :], h2[:, :, 0:H], ALU.subtract))
        p("v1", "pool", 600, ["Q.c_load", "P.av3-", "W.zero_v1_one"], lambda e, b: e.tensor_copy(
            v1[:, :, :, 0:HD], c_in[b.par][:, :, :].rearrange("p t (h d) -> p t h d", d=HD)), kind="scalar")
        def stack(dst, hi, lo):
            def run(e, b):
                return [e.dma_start(
                    dst[32 * block:32 * block + 32, :, :].bitcast(F32).rearrange("p (c r) n -> p r c n", c=C)[:, r],
                    src[32 * r:32 * r + 32, :, :].bitcast(F32)) for block, src in enumerate((hi, lo, hi)) for r in range(4)]
            return run

        q_("c_t", "pe", 500, ["Q.c_load", "P.o_x--", "Q.ks-", "W.ident"],
          turn(lambda c: n_ps[:, 1, c * L:(c + 1) * L], lambda b: c_in[b.par]))
        q_("k_hi", "act", 620, ["Q.c_t"], lambda e, b: e.activation(
            k_hi[:, :, :].rearrange("p a b -> p (a b)"), n_ps[:, 1, :], ACT.Copy))
        q_("k_lo", "dve", 620, ["Q.k_hi"], lambda e, b: e.tensor_tensor(
            k_lo[:, :, :].rearrange("p a b -> p (a b)"), n_ps[:, 1, :],
            k_hi[:, :, :].rearrange("p a b -> p (a b)").bitcast(F32), ALU.subtract))
        q_("ks", "sp", 2500, ["Q.k_lo", "R.k_mm3-"], stack(ks, k_hi, k_lo), 12)
        q_("h_tr", "pe", 250, ["Q.h_lo", "Q.k_lo", "W.ident"], lambda e, b: [
            e.transpose(n_ps[0:2 * H, 1, t * P:(t + 1) * P], h2[:, t, :], ident[:, :]) for t in range(T)][-1], kind="small")
        q_("h_t", "act", 420, ["Q.h_tr", "Q.ks_h-"], lambda e, b: e.activation(
            h_t[:, :], n_ps[0:2 * H, 1, 0:L], ACT.Copy))
        q_("ks_h", "sp", 300, ["Q.h_t", "R.k_mm3-"], lambda e, b: e.dma_start(
            ks[96:P, :, :].bitcast(F32), h_t[:, :].bitcast(F32).unsqueeze(1).to_broadcast([2 * H, PAIRS, L])), True)

        q_("x_t", "pe", 500, ["Q.xn", "P.o_x--", "F.ht_lo--", "Q.qs-"],
          turn(lambda c: n_ps[:, 0, c * L:(c + 1) * L], lambda b: xn))
        q_("q_hi", "act", 620, ["Q.x_t"], lambda e, b: e.activation(
            q_hi[:, :, :].rearrange("p a b -> p (a b)"), n_ps[:, 0, :], ACT.Copy))
        q_("q_lo", "dve", 620, ["Q.q_hi"], lambda e, b: e.tensor_tensor(
            q_lo[:, :, :].rearrange("p a b -> p (a b)"), n_ps[:, 0, :],
            q_hi[:, :, :].rearrange("p a b -> p (a b)").bitcast(F32), ALU.subtract))
        q_("qs", "sp", 2500, ["Q.q_lo", "R.q_mm3-"], stack(qs, q_hi, q_lo), 12)

        def features(src, rows, n, bank):
            def run(e, b):
                for half in range(2):
                    pr = 2 * n + half
                    last = e.matmul(p_ps[:, bank, half * L:(half + 1) * L], wf[0:rows, pr, :],
                                    src[0:rows, pr, :], start=True, stop=True)
                return last
            return run

        def r_(name, eng, ns, waits, run, dma=False, kind=""):
            Rn.append(Step(name, eng, ns, waits, run, dma, kind))

        for key, src, rows_in, dst in (("q", qs, 96, qf), ("k", ks, P, kf)):
            for n in range(4):
                bank, free = P_BANKS[f"{key}_exp{n}"]
                r_(f"{key}_mm{n}", "pe", 250, [f"Q.{key}s", free, "W.wf"] + (["Q.ks_h"] if key == "k" else []),
                  features(src, rows_in, n, bank))
                flat = dst[:, 2 * n:2 * n + 2, :].rearrange("p a b -> p (a b)")
                r_(f"{key}_exp{n}", "act", 620, [f"R.{key}_mm{n}", f"P.a_mm_diag1{n | 1}-"],
                  lambda e, b, bank=bank, flat=flat: e.activation(flat, p_ps[:, bank, :], ACT.Exp))
                r_(f"{key}f{n}", "pool", 600, [f"R.{key}_exp{n}"],
                  lambda e, b, flat=flat: e.tensor_scalar(flat, flat, KERNEL_EPS, 1.0, ALU.add, ALU.mult), kind="scalar")

        def head(q, j):
            return 8 * (q // 2) + 2 * j + q % 2

        def scores(q, bank, tk, tq):
            def run(e, b):
                for j in range(4):
                    pr, half = divmod(head(q, j), 2)
                    rows_ = slice(M * half, M * half + M)
                    last = e.matmul(p_ps[:, bank, j * P:(j + 1) * P],
                                    kf[rows_, pr, tk * P:(tk + 1) * P],
                                    qf[rows_, pr, tq * P:(tq + 1) * P], start=True, stop=True)
                return last
            return run

        def av(q):
            def run(e, b):
                bank, col = divmod(q * L, 512)
                for part in range(2):
                    for j in range(4):
                        h = head(q, j)
                        out = n_ps[32 * j:32 * j + 32, bank, col + part * P:col + L]
                        a = att[q % 2][:, j, 2 * part * P:2 * P + part * P]
                        last = e.matmul(out, v1[:, part, h, :], a, start=(part == 0), stop=(part == 1),
                                        skip_group_check=True, tile_position=(0, 32 * j))
                return last
            return run

        for q in range(QUADS):
            banks = []
            for kind, tk, tq in (("diag0", 0, 0), ("cross", 0, 1), ("diag1", 1, 1)):
                bank, free = P_BANKS[f"a_{kind}{q}"]
                banks.append(bank)
                p(f"a_mm_{kind}{q}", "pe", 900, [free, f"R.qf{q | 1}", f"R.kf{q | 1}"], scores(q, bank, tk, tq))
            reader = f"P.av{q - 2}" if q >= 2 else f"P.av{q + 2}-"
            mask = causal[:, :].unsqueeze(1).to_broadcast([P, 4, P])

            def masked(q, bank, col):
                return lambda e, b: e.tensor_tensor(
                    att[q % 2][:, :, col:col + P],
                    p_ps[:, bank, :].rearrange("p (j l) -> p j l", j=4), mask, ALU.mult)

            p(f"a_diag0{q}", "dve", 620, [f"P.a_mm_diag0{q}", reader, "W.tri"], masked(q, banks[0], 0))
            p(f"a_cross{q}", "act", 620, [f"P.a_mm_cross{q}", reader], lambda e, b, q=q, bank=banks[1]: e.activation(
                att[q % 2][:, :, P:2 * P], p_ps[:, bank, :].rearrange("p (j l) -> p j l", j=4), ACT.Copy))
            p(f"a_diag1{q}", "dve", 620, [f"P.a_mm_diag1{q}", reader], masked(q, banks[2], 2 * P))
            if q:
                p(f"av{q - 1}", "pe", 650, [f"P.a_diag1{q - 1}", f"P.a_cross{q - 1}", "P.v1", "Q.q_lo+", "Q.h_t+", "F.ht_lo-"],
                  av(q - 1))
        p(f"av{QUADS - 1}", "pe", 650, [f"P.a_diag1{QUADS - 1}", f"P.a_cross{QUADS - 1}"], av(QUADS - 1))

        for half in range(2):
            p(f"nt{half}", "act", 620, [f"P.av{2 * half + 1}", "P.nt_t-"], lambda e, b, half=half: e.activation(
                nt[:, 2 * half:2 * half + 2, :].rearrange("p a b -> p (a b)"), n_ps[:, half, :], ACT.Copy))
        p("nt_t", "pe", 1000, ["P.nt0", "P.nt1"], lambda e, b: [
            e.transpose(n_ps[:, t, :].rearrange("p (a j s v) -> p a s j v", a=2, s=2, v=32)[:, q // 2, q % 2],
                        nt[:, q, t * P:(t + 1) * P], ident[:, :])
            for t in range(T) for q in range(QUADS)][-1])
        nd = n_ps[:, :, :].rearrange("p t (h v) -> p t h v", v=32)
        p("den_small", "dve", 100, ["P.nt_t", "P.den-"], lambda e, b: e.tensor_scalar(
            den3[:, 0], nd[:, :, :, HD], M * NORM_STAB, None, ALU.is_le))
        p("den", "dve", 100, ["P.den_small"], lambda e, b: e.scalar_tensor_tensor(
            out=den3[:, 1], in0=den3[:, 0], scalar=2.0 * M * NORM_STAB, in1=nd[:, :, :, HD],
            op0=ALU.mult, op1=ALU.add))
        p("recip", "dve", 100, ["P.den"], lambda e, b: e.reciprocal(den3[:, 2], den3[:, 1]))
        p("o_x", "dve", 620, ["P.recip"], lambda e, b: [e.tensor_tensor(
            o_x[:, t, :].rearrange("p (h d) -> p h d", d=HD), nd[:, t, :, 0:HD],
            den3[:, 2, t, :].unsqueeze(2).to_broadcast([P, H, HD]), ALU.mult) for t in range(T)][-1])
        p("x1", "dve", 620, ["P.o_x", "Q.x_load", "E.out--", "W.tanh"], lambda e, b: e.scalar_tensor_tensor(
            out=x1[b.par][:, :, :], in0=o_x[:, :, :], scalar=tanh_x[:, 0:1], in1=x_in[b.par][:, :, :],
            op0=ALU.mult, op1=ALU.add))

        w("zero_v1", "dve", [], lambda e, b: e.memset(v1[:, :, :, :], 0.0))
        w("zero_v1_one", "dve", ["W.zero_v1"], lambda e, b: e.memset(v1[:, :, :, HD:HD + 1], 1.0))

        Fn = []
        def f(name, eng, ns, waits, run, dma=False, kind=""):
            Fn.append(Step(name, eng, ns, waits, run, dma, kind))

        Gn = []

        def g(name, eng, ns, waits, run, dma=False, kind=""):
            Gn.append(Step(name, eng, ns, waits, run, dma, kind))

        g("bn", "dve", 700, ["P.x1", "G.bn_agg-"], lambda e, b: [
            e.bn_stats(bn6g[:, t, :], x1[b.par][:, t, :]) for t in range(T)][-1])
        g("bn_agg", "dve", 150, ["G.bn", "G.hn-"], lambda e, b: [
            e.bn_aggr(mvg[:, t, :], bn6g[:, t, :]) for t in range(T)][-1], kind="aggr")
        g("var", "dve", 140, ["G.bn_agg", "G.rstd-"], lambda e, b: (
            e.tensor_scalar(var_f[:, 0, :], mvg[:, :, 1], LN_EPS, None, ALU.add),
            e.tensor_scalar(var_f[:, 1, :], mvg[:, :, 1], 1.0 + RMS_EPS, RMS_EPS * LN_EPS,
                            ALU.mult, ALU.add))[1])
        g("rstd", "pool", 300, ["G.var", "G.hn-"], lambda e, b: e.tensor_tensor(
            r_f[:, :, :].rearrange("p a b -> p (a b)"), var_f[:, :, :].rearrange("p a b -> p (a b)"),
            neg_half[:, 0:2 * T], ALU.pow))
        def norm(dst, which):
            return lambda e, b: [e.tensor_scalar(
                dst[:, t, :], x1[b.par][:, t, :], mvg[:, t, 0:1], r_f[:, which, t:t + 1],
                ALU.subtract, ALU.mult) for t in range(T)][-1]
        g("hn", "dve", 450, ["G.rstd", "F.h_t-"], norm(hn, 1))
        g("y", "dve", 450, ["G.rstd", "G.yb-"], norm(y, 0))
        A_bo = b_o[:, :].unsqueeze(1).to_broadcast([P, T, D])
        g("yb", "pool", 1200, ["G.y", "F.y2-", "W.ld_bo"], lambda e, b: e.tensor_tensor(
            yb[:, :, :], y[:, :, :], A_bo, ALU.add))

        def turn_c(name, src, waits, hi, lo, readers):
            for c in range(C):
                bank, free = F_BANKS[f"{readers}{c}"]
                f(f"{name}{c}", "pe", 250, waits + [free], lambda e, b, c=c, bank=bank: [
                    e.transpose(f_ps[:, bank, t * P:(t + 1) * P], src[:, t, c * P:(c + 1) * P],
                                ident[:, :]) for t in range(T)][-1])
                f(f"{name}_hi{c}", "act", 400, [f"F.{name}{c}", "E.e_mm1_3-"], lambda e, b, c=c, bank=bank:
                  e.activation(hi[:, c, :], f_ps[:, bank, 0:L], ACT.Copy))
                f(f"{readers}{c}", "dve", 380, [f"F.{name}_hi{c}", "E.e_mm1_3-"], lambda e, b, c=c, bank=bank:
                  e.tensor_tensor(lo[:, c, :], f_ps[:, bank, 0:L], hi[:, c, :].bitcast(F32), ALU.subtract))

        def three_passes(e, out, a_hi, a_lo, b_hi, b_lo):
            for c in range(C):
                e.matmul(out, a_hi(c), b_hi(c), start=(c == 0), stop=False)
                e.matmul(out, a_hi(c), b_lo(c), start=False, stop=False)
                last = e.matmul(out, a_lo(c), b_hi(c), start=False, stop=(c == C - 1))
            return last

        def tok(tile, t):
            return lambda c: tile[:, c, t * P:(t + 1) * P]

        def cols(tile, a, b_):
            return lambda c: tile[:, c, a:b_]

        f("h_t", "pe", 500, ["G.hn", "P.o_x"], turn(lambda c: n_ps[:, 0, c * L:(c + 1) * L], lambda b: hn))
        f("ht_hi", "act", 620, ["F.h_t", "F.v_mm-"], lambda e, b: e.activation(
            ht_hi[:, :, :].rearrange("p a b -> p (a b)"), n_ps[:, 0, :], ACT.Copy))
        f("ht_lo", "dve", 620, ["F.ht_hi", "F.v_mm-"], lambda e, b: e.tensor_tensor(
            ht_lo[:, :, :].rearrange("p a b -> p (a b)"), n_ps[:, 0, :],
            ht_hi[:, :, :].rearrange("p a b -> p (a b)").bitcast(F32), ALU.subtract))

        for t in range(T):
            bank, free = F_BANKS[f"qk{t}"]
            f(f"qk_mm{t}", "pe", 1370, ["F.ht_lo", free, "W.wqkv_lo"], lambda e, b, t=t, bank=bank: three_passes(
                e, f_ps[:, bank, :], tok(ht_hi, t), tok(ht_lo, t),
                cols(wqkv_hi, 0, 2 * D), cols(wqkv_lo, 0, 2 * D)))
            f(f"qk{t}", "dve", 620, [f"F.qk_mm{t}", "F.k_t-", "W.bkv_sb", "W.ld_bq"], lambda e, b, t=t, bank=bank:
              e.tensor_tensor(qkv[:, t, 0:2 * D], f_ps[:, bank, :], b_qkv[:, 0:2 * D], ALU.add))
        bank, free = F_BANKS["vv"]

        def v_mm(e, b, bank=bank):
            for t in range(T):
                last = three_passes(e, f_ps[:, bank, t * D:(t + 1) * D], tok(ht_hi, t), tok(ht_lo, t),
                                    cols(wqkv_hi, 2 * D, 3 * D), cols(wqkv_lo, 2 * D, 3 * D))
            return last

        f("v_mm", "pe", 1440, [free], v_mm)
        f("vv", "dve", 620, ["F.v_mm", "F.v_t-"], lambda e, b, bank=bank: e.tensor_tensor(
            qkv[:, :, 2 * D:3 * D], f_ps[:, bank, :].rearrange("p (t n) -> p t n", t=T),
            b_qkv[:, 2 * D:3 * D].unsqueeze(1).to_broadcast([P, T, D]), ALU.add))

        def in_parts(name, ns, waits, run, bank):
            for part in range(PARTS):
                f(name if part == PARTS - 1 else f"{name}{part}", "pe", ns, [] if part else waits,
                  lambda e, b, part=part: run(e, bank, part), kind="small")

        def heads_of(a):
            return qkv[:, :, a:a + D].rearrange("p t (h d) -> p h t d", d=HD)

        f("q_t", "dve", 620, ["F.qk1", "F.q_bd-"], lambda e, b: e.transpose(q_t[:, :, :], heads_of(0)))
        f("q_bd", "dve", 650, ["F.q_t", "F.s_mm-", "W.sel_tok"], lambda e, b: [e.tensor_scalar(
            q_bd[:, t, :, :], q_t[:, :, :], sel_tok[:, t:t + 1], None, ALU.mult) for t in range(T)][-1])
        f("k_t", "dve", 620, ["F.qk1", "F.s_mm-"], lambda e, b: e.transpose(k_t[:, :, :], heads_of(D)))

        bank, free = F_BANKS["s_sub"]

        def s_mm(e, bank, part):
            for n in range(32 * part // PARTS, 32 * (part + 1) // PARTS):
                for j in range(4):
                    r = slice(32 * j, 32 * j + 32)
                    last = e.matmul(f_ps[r, bank, n * H:(n + 1) * H], q_bd[r, :, :, n], k_t[r, :, n],
                                    start=True, stop=True, tile_position=(32 * j, 32 * j))
            return last

        in_parts("s_mm", 1450, ["F.q_bd", "F.k_t", free], s_mm, bank)
        f("v_t", "dve", 620, ["F.vv", "F.pv-"], lambda e, b: e.transpose(
            v_t[:, :, :], qkv[:, :, 2 * D:3 * D].rearrange("p t (g d) -> p d t g", d=HD)))
        sc = f_ps[:, bank, :].rearrange("p (n g) -> p n g", g=H)

        def per_row(tile):
            return tile[:, :].unsqueeze(2).to_broadcast([P, 32, H])

        f("s_max", "dve", 620, ["F.s_mm", "F.s_sub-"], lambda e, b: e.tensor_reduce(
            s_max[:, :], sc, AX.X, ALU.max))
        f("s_sub", "dve", 620, ["F.s_max", "F.s_exp-"], lambda e, b: e.tensor_tensor(
            s_sub[:, :, :], sc, per_row(s_max), ALU.subtract))
        f("s_exp", "act", 620, ["F.s_sub", "F.s_norm-"], lambda e, b: e.activation(
            s_exp[:, :, :], s_sub[:, :, :], ACT.Exp, scale=float(HD) ** -0.5))
        f("s_sum", "dve", 620, ["F.s_exp"], lambda e, b: e.tensor_reduce(
            s_sum[:, :], s_exp[:, :, :], AX.X, ALU.add))
        f("s_rec", "dve", 90, ["F.s_sum"], lambda e, b: e.reciprocal(s_rec[:, :], s_sum[:, :]))
        f("s_norm", "dve", 620, ["F.s_rec"], lambda e, b: e.tensor_tensor(
            s_exp[:, :, :], s_exp[:, :, :], per_row(s_rec), ALU.mult))
        f("p_bd", "dve", 650, ["F.s_norm"], lambda e, b: [e.tensor_scalar(
            p_bd[:, :, t, :], s_exp[:, :, :], sel_tok[:, t:t + 1], None, ALU.mult) for t in range(T)][-1])
        f("p_t", "dve", 1150, ["F.p_bd", "F.pv-"], lambda e, b: e.transpose(
            p_t[:, :, :], p_bd[:, :, :, :].rearrange("p n t g -> p n (t g)")))
        bank, free = F_BANKS["o_tok"]

        def pv(e, bank, part):
            for n in range(32 * part // PARTS, 32 * (part + 1) // PARTS):
                for j in range(4):
                    r = slice(32 * j, 32 * j + 32)
                    last = e.matmul(f_ps[r, bank, n * HD:(n + 1) * HD], p_t[r, n, :], v_t[r, :, n],
                                    start=True, stop=True, tile_position=(32 * j, 32 * j))
            return last

        in_parts("pv", 1450, ["F.p_t", "F.v_t", free], pv, bank)
        f("o_tok", "dve", 620, ["F.pv", "F.o_tr-"], lambda e, b, bank=bank: e.transpose(
            o_tok[:, :, :].rearrange("p t (h d) -> p d t h", d=HD),
            f_ps[:, bank, :].rearrange("p (n d) -> p d n", d=HD)))

        bank, free = F_BANKS["ot_lo"]
        f("o_tr", "pe", 500, ["F.o_tok", free], lambda e, b, bank=bank: [
            e.transpose(f_ps[:, bank, c * L + t * P:c * L + (t + 1) * P], o_tok[:, t, c * P:(c + 1) * P],
                        ident[:, :]) for c in range(C) for t in range(T)][-1])
        f("ot_hi", "act", 620, ["F.o_tr"], lambda e, b, bank=bank: e.activation(
            ot_hi[:, :, :].rearrange("p a b -> p (a b)"), f_ps[:, bank, :], ACT.Copy))
        f("ot_lo", "dve", 620, ["F.ot_hi"], lambda e, b, bank=bank: e.tensor_tensor(
            ot_lo[:, :, :].rearrange("p a b -> p (a b)"), f_ps[:, bank, :],
            ot_hi[:, :, :].rearrange("p a b -> p (a b)").bitcast(F32), ALU.subtract))
        bank, free = F_BANKS["y2"]

        def o_mm(e, b, bank=bank):
            for t in range(T):
                last = three_passes(e, f_ps[:, bank, t * D:(t + 1) * D], tok(ot_hi, t), tok(ot_lo, t),
                                    cols(wo_hi, 0, D), cols(wo_lo, 0, D))
            return last

        f("o_mm", "pe", 1440, ["F.ot_lo", free, "W.wo_lo"], o_mm)
        f("y2", "dve", 620, ["F.o_mm", "G.yb", "E.e0_0a-", "E.e1_0a-", "F.h2n-"], lambda e, b, bank=bank:
          e.tensor_tensor(y2[:, :, :], f_ps[:, bank, :].rearrange("p (t n) -> p t n", t=T),
                          yb[:, :, :], ALU.add))
        f("bn2", "dve", 700, ["F.y2", "F.bn2_agg-"], lambda e, b: [
            e.bn_stats(bn6f[:, t, :], y2[:, t, :]) for t in range(T)][-1])
        f("bn2_agg", "dve", 150, ["F.bn2"], lambda e, b: [
            e.bn_aggr(mvf[:, t, :], bn6f[:, t, :]) for t in range(T)][-1], kind="aggr")
        f("ms0", "dve", 70, ["F.bn2_agg", "F.ms-"], lambda e, b: e.tensor_tensor(
            sq[:, :], mvf[:, :, 0], mvf[:, :, 0], ALU.mult))
        f("ms", "dve", 70, ["F.ms0", "F.r2-"], lambda e, b: e.scalar_tensor_tensor(
            out=ms[:, :], in0=sq[:, :], scalar=RMS_EPS, in1=mvf[:, :, 1], op0=ALU.add, op1=ALU.add))
        f("r2", "pool", 300, ["F.ms", "F.h2n-"], lambda e, b: e.tensor_tensor(
            r2[:, :], ms[:, :], neg_half[:, 0:T], ALU.pow))
        f("h2n", "dve", 450, ["F.r2", "F.h2_t1-"], lambda e, b: [e.tensor_scalar(
            h2n[:, t, :], y2[:, t, :], r2[:, t:t + 1], None, ALU.mult) for t in range(T)][-1])
        turn_c("h2_t", h2n, ["F.h2n"], h2_hi, h2_lo, "h2_lo")

        En = []

        def e_(name, eng, ns, waits, run, dma=False, kind=""):
            En.append(Step(name, eng, ns, waits, run, dma, kind))

        e_("g_mm", "pe", 730, ["F.h2_lo1", "E.e1_3b-", "W.wg_lo"], lambda e, b: three_passes(
            e, e_ps[:, 0:L], lambda c: wg_hi[:, c, :], lambda c: wg_lo[:, c, :],
            lambda c: h2_hi[:, c, :], lambda c: h2_lo[:, c, :]))
        e_("gl", "act", 420, ["E.g_mm", "E.g_t-"], lambda e, b: e.activation(
            gl[:, :], e_ps[0:E, 0:L], ACT.Copy))

        e_("g_t", "pe", 150, ["E.gl"], lambda e, b: [
            e.transpose(e_ps[:, L + t * E:L + (t + 1) * E], gl[:, t * P:(t + 1) * P], ident[0:E, 0:E])
            for t in range(T)][-1], kind="small")
        e_("ga", "dve", 90, ["E.g_t", "E.gb-", "W.ld_bg"], lambda e, b: e.tensor_tensor(
            ga[:, :, :], e_ps[:, L:L + T * E].rearrange("p (t e) -> p t e", t=T),
            b_g[:, :].unsqueeze(1).to_broadcast([P, T, E]), ALU.add))
        e_("gmax", "dve", 90, ["E.ga", "E.gate-"], lambda e, b: e.tensor_reduce(gm[:, :], ga[:, :, :], AX.X, ALU.max))
        e_("gb", "dve", 90, ["E.gmax", "E.gexp-"], lambda e, b: e.tensor_tensor(
            gb[:, :, :], ga[:, :, :], gm[:, :].unsqueeze(2).to_broadcast([P, T, E]), ALU.subtract))
        e_("gexp", "act", 250, ["E.gb", "E.e1_3b-"], lambda e, b: e.activation(
            gate[:, :, :], gb[:, :, :], ACT.Exp))
        e_("gsum", "dve", 90, ["E.gexp"], lambda e, b: e.tensor_reduce(gm[:, :], gate[:, :, :], AX.X, ALU.add))
        e_("grec", "dve", 90, ["E.gsum"], lambda e, b: e.reciprocal(gr[:, :], gm[:, :]))
        e_("gate", "dve", 90, ["E.grec"], lambda e, b: e.tensor_tensor(
            gate[:, :, :], gate[:, :, :], gr[:, :].unsqueeze(2).to_broadcast([P, T, E]), ALU.mult))

        for t in range(T):
            for n in range(E // 2):
                free = f"E.e{t}_{n - 1}b" if n else ("E.e0_3b" if t else "E.ga")
                e_(f"e_mm{t}_{n}", "pe", 1370, ["F.h2_lo1", free, "W.we_lo"], lambda e, b, t=t, n=n:
                   three_passes(e, e_ps[:, :], tok(h2_hi, t), tok(h2_lo, t),
                                cols(we_hi, 2 * n * D, 2 * (n + 1) * D), cols(we_lo, 2 * n * D, 2 * (n + 1) * D)))
                for half in range(2):
                    ex = 2 * n + half
                    src = y2[:, t, :] if ex == 0 else acc[t][(ex - 1) % 2][:, :]
                    before = "E.gate" if ex == 0 else f"E.e{t}_{(ex - 1) // 2}{'ab'[(ex - 1) % 2]}"
                    waits = [f"E.e_mm{t}_{n}", before] + (["E.out-"] if ex == 1 else [])
                    e_(f"e{t}_{n}{'ab'[half]}", "dve", 400, waits, lambda e, b, t=t, ex=ex, half=half, src=src:
                       e.scalar_tensor_tensor(out=acc[t][ex % 2][:, :], in0=e_ps[:, half * D:(half + 1) * D],
                                              scalar=gate[:, t, ex:ex + 1], in1=src, op0=ALU.mult, op1=ALU.add))
        e_("out", "dve", 800, ["E.e0_3b", "E.e1_3b", "E.store-", "W.tanh"], lambda e, b: [
            e.scalar_tensor_tensor(out=outb[:, t, :], in0=acc[t][1][:, :], scalar=tanh_f[:, 0:1],
                                   in1=x1[b.par][:, t, :], op0=ALU.mult, op1=ALU.add) for t in range(T)][-1])
        e_("store", "sp", 50, ["E.out"], lambda e, b: e.dma_start(
            out_d[bass.ds(b.times(1), 1), :, :].rearrange("b (t p) d -> p (b t) d", p=P),
            outb[:, :, :]), True)

        def phase(st):
            return 0 if st.dma or st.eng == "pool" or st.name.startswith("zero") else 1 if st.name in BEFORE_Q else 2

        W.sort(key=phase)
        for key, steps in (("W", W), ("A", A), ("S", S), ("Q", Qn), ("R", Rn), ("P", Pn), ("G", Gn), ("F", Fn), ("E", En)):
            streams[key] = Stream(key, steps, sem)

        names = {"pe": "tensor", "act": "scalar", "dve": "vector", "pool": "gpsimd", "sp": "sync"}
        body_order = in_order([("Q", Qn), ("R", Rn), ("P", Pn), ("G", Gn), ("F", Fn), ("E", En)])

        def emit(eng_key, eng, key, steps, batch):
            for st in steps:
                if st.eng == eng_key:
                    streams[key].emit(st, eng, batch, streams)

        def program(eng_key, eng):
            emit(eng_key, eng, "W", [st for st in W if phase(st) == 0], Batch(0, 0))
            for k in range(2):
                emit(eng_key, eng, "A", A, Batch(0, k))
            if eng_key in ("sp", "act", "dve"):
                with eng.Fori(1, NB // CH // 2) as i:
                    for k in range(2):
                        emit(eng_key, eng, "A", A, Batch(i, k))
            emit(eng_key, eng, "W", [st for st in W if phase(st) == 1], Batch(0, 0))
            emit(eng_key, eng, "S", S, Batch(0, 0))

            def body(i, k, keys="QRPGFE"):
                for key, st in body_order:
                    if st.eng == eng_key and key in keys:
                        streams[key].emit(st, eng, Batch(i, k + AHEAD[key]), streams)

            body(0, -1, "QR")
            emit(eng_key, eng, "W", [st for st in W if phase(st) == 2], Batch(0, 0))
            body(0, 0, "QRPG")
            body(0, 1, "QRPGF")
            body(0, 2)
            with eng.Fori(0, (NB - 4) // 2) as i:
                body(i, 3)
                body(i, 4)
            last_i = (NB - 4) // 2
            body(last_i, 3, "PGFE")
            body(last_i, 4, "FE")
            body(last_i, 5, "E")
            if eng_key == "sp":
                for par in range(2):
                    st_sem, per_i, value = streams["E"].target("store", Batch(0, par))
                    eng.wait_ge(st_sem, (NB - 2) // 2 * per_i + value)

        streams["A"].place["end"] = streams["A"].place["sum"]
        end_steps = Step("end", "dve", 0, [], None)
        streams["A"].by_name["end"] = end_steps
        plain = streams["A"].target

        def a_target(name, batch):
            if name != "end":
                return plain(name, batch)
            sem_, _, value = plain("sum", Batch(0, last_chunk))
            return sem_, 0, value

        streams["A"].target = a_target

        block = ctx.enter_context(nc.Block())

        @block.sync
        def _(eng):
            program("sp", eng)

        @block.gpsimd
        def _(eng):
            program("pool", eng)

        @block.scalar
        def _(eng):
            program("act", eng)

        @block.vector
        def _(eng):
            program("dve", eng)

        @block.tensor
        def _(eng):
            program("pe", eng)


_INS = ['x', 'ctx_1024', 'g_xattn', 'g_ffn', 'L0_xattn_random_features', 'L0_ffn_gamma1', 'L0_ffn_Wq',
        'L0_ffn_bq', 'L0_ffn_Wdown', 'L0_ffn_bdown', 'L0_ffn_Wup', 'L0_ffn_bup', 'L0_ffn_Wo', 'L0_ffn_bo',
        'L0_ffn_gamma2', 'L0_ffn_Wg', 'L0_ffn_bg', 'L0_ffn_We']


def kernel(**inputs):
    import numpy as _np
    import concourse.bacc as _bacc
    from concourse import mybir as _mybir
    from concourse.bass_utils import run_bass_kernel_spmd as _run

    nc = _bacc.Bacc("TRN2", target_bir_lowering=False, num_devices=1)
    arrays, args = {}, []
    for name in _INS:
        a = _np.ascontiguousarray(inputs[name])
        arrays[f"in_{name}"] = a
        args.append(nc.dram_tensor(f"in_{name}", a.shape, _mybir.dt.from_np(a.dtype), kind="ExternalInput").ap())
    args.append(nc.dram_tensor("out_0", (NB, L, D), F32, kind="ExternalOutput").ap())
    build(nc, *args)
    r = _run(nc, [arrays], core_ids=[0])
    return r.results[0]["out_0"]
```
